# Optimizing a Trainium2 kernel written in Bass

```python
import numpy as np
import jax
import jax.numpy as jnp

def _softmax(x, axis=-1):
    return jax.nn.softmax(x, axis=axis)

def _gelu(x):
    return jax.nn.gelu(x, approximate=True)

def _silu(x):
    return jax.nn.silu(x)

def _sigmoid(x):
    return jax.nn.sigmoid(x)

def _layernorm(x, axis=-1, eps=1e-05):
    m = jnp.mean(x, axis=axis, keepdims=True)
    v = jnp.var(x, axis=axis, keepdims=True)
    return (x - m) / jnp.sqrt(v + eps)

def _scatter_add(tgt, idx, src, axis=0):
    return tgt.at[idx].add(src)

def _segment_sum(src, seg, n):
    return jax.ops.segment_sum(src, seg, n)
kernel_name = 'mk_gnn_resnorm_d2_gnn_r8_26290f'

def setup_inputs(seed: int=0):
    np.random.seed(seed)
    _w = jnp.asarray

    def _rec_inputs():
        import jax
        import jax.numpy as jnp
        _gk = jax.random.key(seed)
        x = -0.0001126 + 1 * jax.random.normal(jax.random.fold_in(_gk, 1), (1250, 768), jnp.float32)
        src = jax.random.randint(jax.random.fold_in(_gk, 2), (40000,), 0, 1250, jnp.int32)
        dst = jax.random.randint(jax.random.fold_in(_gk, 3), (40000,), 0, 1250, jnp.int32)
        _o = jnp.argsort(dst, stable=True)
        src = src[_o]
        dst = dst[_o]
        edge_type_3 = jax.random.randint(jax.random.fold_in(_gk, 12), (40000,), 0, 3, jnp.int32)
        return (x, src, dst, edge_type_3)
    x, src, dst, edge_type_3 = _rec_inputs()

    def _L0_gnn_setup():
        import jax, jax.numpy as jnp
        import numpy as np
        N = 1250
        E = 20000
        D = 768
        H1, C1 = (4, 192)
        H2, C2 = (2, 96)
        EPS = 1e-05
        NEG_SLOPE = 0.2

        def layer_norm(x, g, b):
            mu = x.mean(-1, keepdims=True)
            var = ((x - mu) ** 2).mean(-1, keepdims=True)
            return (x - mu) * jax.lax.rsqrt(var + EPS) * g + b

        def gat_conv(x, src, dst, W, a_src, a_dst, bias, H, C, n):
            h = (x @ W).reshape(n, H, C)
            s_src = (h * a_src).sum(-1)
            s_dst = (h * a_dst).sum(-1)
            e = jax.nn.leaky_relu(s_src[src] + s_dst[dst], NEG_SLOPE)
            emax = jax.ops.segment_max(e, dst, num_segments=n)
            ee = jnp.exp(e - emax[dst])
            denom = jax.ops.segment_sum(ee, dst, num_segments=n)
            alpha = ee / denom[dst]
            out = jax.ops.segment_sum(alpha[:, :, None] * h[src], dst, num_segments=n)
            return out.reshape(n, H * C) + bias
        key = jax.random.key(seed)
        ks = jax.random.split(key, 16)
        sd = 1.0 / np.sqrt(D)
        inp = {'x': jax.random.normal(ks[0], (N, D), jnp.float32), 'edge_index': jax.random.randint(ks[1], (2, E), 0, N, jnp.int64), 'norm_g': jnp.ones((D,), jnp.float32), 'norm_b': jnp.zeros((D,), jnp.float32), 'W1': jax.random.normal(ks[2], (D, H1 * C1), jnp.float32) * sd, 'a_src1': jax.random.normal(ks[3], (H1, C1), jnp.float32) * sd, 'a_dst1': jax.random.normal(ks[4], (H1, C1), jnp.float32) * sd, 'b1': jnp.zeros((H1 * C1,), jnp.float32), 'W2': jax.random.normal(ks[5], (H1 * C1, H2 * C2), jnp.float32) * sd, 'a_src2': jax.random.normal(ks[6], (H2, C2), jnp.float32) * sd, 'a_dst2': jax.random.normal(ks[7], (H2, C2), jnp.float32) * sd, 'b2': jnp.zeros((H2 * C2,), jnp.float32), 'Wu': jax.random.normal(ks[8], (D + H2 * C2, D), jnp.float32) / np.sqrt(D + H2 * C2), 'bu': jnp.zeros((D,), jnp.float32)}
        return inp
    _L0_gnn_all = _L0_gnn_setup()
    _L0_gnn_in = {k: v for k, v in _L0_gnn_all.items() if k in ('norm_g', 'norm_b', 'W1', 'a_src1', 'a_dst1', 'b1', 'W2', 'a_src2', 'a_dst2', 'b2', 'Wu', 'bu')}
    del _L0_gnn_all

    def _L1_gnn_setup():
        import jax, jax.numpy as jnp
        import numpy as np
        NEG_SLOPE = 0.2
        EPS = 1e-16
        N_NODES = 4096
        N_EDGES = 20000
        DIM = 768
        HEADS1 = 4
        OUT1 = DIM // HEADS1
        HEADS2 = 1
        OUT2 = DIM
        N_REL = 3

        def rgat_conv(x, W, q, k, b, src, dst, etype, heads, out_ch, n_nodes):
            xr = jnp.einsum('nd,rdf->rnf', x, W)
            oi = xr[etype, dst]
            oj = xr[etype, src]
            qi = oi @ q
            kj = oj @ k
            alpha = jax.nn.leaky_relu(qi + kj, NEG_SLOPE)
            m = jax.ops.segment_max(alpha, dst, num_segments=n_nodes)
            e = jnp.exp(alpha - m[dst])
            z = jax.ops.segment_sum(e, dst, num_segments=n_nodes)
            a = e / (z[dst] + EPS)
            msg = (a[:, :, None] * oj.reshape(-1, heads, out_ch)).reshape(-1, heads * out_ch)
            out = jax.ops.segment_sum(msg, dst, num_segments=n_nodes)
            return out + b
        key = jax.random.key(seed)
        ks = jax.random.split(key, 12)
        s = 0.02
        return {'x': jax.random.normal(ks[0], (N_NODES, DIM), dtype=jnp.float32), 'edge_index': jax.random.randint(ks[1], (2, N_EDGES), 0, N_NODES, dtype=jnp.int64), 'edge_type': jax.random.randint(ks[2], (N_EDGES,), 0, N_REL, dtype=jnp.int64), 'W1': jax.random.normal(ks[3], (N_REL, DIM, HEADS1 * OUT1), dtype=jnp.float32) * s, 'q1': jax.random.normal(ks[4], (HEADS1 * OUT1, HEADS1), dtype=jnp.float32) * s, 'k1': jax.random.normal(ks[5], (HEADS1 * OUT1, HEADS1), dtype=jnp.float32) * s, 'b1': jnp.zeros((HEADS1 * OUT1,), dtype=jnp.float32), 'W2': jax.random.normal(ks[6], (N_REL, DIM, HEADS2 * OUT2), dtype=jnp.float32) * s, 'q2': jax.random.normal(ks[7], (HEADS2 * OUT2, HEADS2), dtype=jnp.float32) * s, 'k2': jax.random.normal(ks[8], (HEADS2 * OUT2, HEADS2), dtype=jnp.float32) * s, 'b2': jnp.zeros((HEADS2 * OUT2,), dtype=jnp.float32)}
    _L1_gnn_all = _L1_gnn_setup()
    _L1_gnn_in = {k: v for k, v in _L1_gnn_all.items() if k in ('W1', 'q1', 'k1', 'b1', 'W2', 'q2', 'k2', 'b2')}
    del _L1_gnn_all
    return {'x': x, 'src': src, 'dst': dst, 'edge_type_3': edge_type_3, 'L0_gnn_norm_g': _L0_gnn_in['norm_g'], 'L0_gnn_norm_b': _L0_gnn_in['norm_b'], 'L0_gnn_W1': _L0_gnn_in['W1'], 'L0_gnn_a_src1': _L0_gnn_in['a_src1'], 'L0_gnn_a_dst1': _L0_gnn_in['a_dst1'], 'L0_gnn_b1': _L0_gnn_in['b1'], 'L0_gnn_W2': _L0_gnn_in['W2'], 'L0_gnn_a_src2': _L0_gnn_in['a_src2'], 'L0_gnn_a_dst2': _L0_gnn_in['a_dst2'], 'L0_gnn_b2': _L0_gnn_in['b2'], 'L0_gnn_Wu': _L0_gnn_in['Wu'], 'L0_gnn_bu': _L0_gnn_in['bu'], 'L1_gnn_W1': _L1_gnn_in['W1'], 'L1_gnn_q1': _L1_gnn_in['q1'], 'L1_gnn_k1': _L1_gnn_in['k1'], 'L1_gnn_b1': _L1_gnn_in['b1'], 'L1_gnn_W2': _L1_gnn_in['W2'], 'L1_gnn_q2': _L1_gnn_in['q2'], 'L1_gnn_k2': _L1_gnn_in['k2'], 'L1_gnn_b2': _L1_gnn_in['b2']}

def reference(x, src, dst, edge_type_3, L0_gnn_norm_g, L0_gnn_norm_b, L0_gnn_W1, L0_gnn_a_src1, L0_gnn_a_dst1, L0_gnn_b1, L0_gnn_W2, L0_gnn_a_src2, L0_gnn_a_dst2, L0_gnn_b2, L0_gnn_Wu, L0_gnn_bu, L1_gnn_W1, L1_gnn_q1, L1_gnn_k1, L1_gnn_b1, L1_gnn_W2, L1_gnn_q2, L1_gnn_k2, L1_gnn_b2):
    import jax
    import jax.numpy as jnp

    def _L0_gnn_ref(x, edge_index, norm_g, norm_b, W1, a_src1, a_dst1, b1, W2, a_src2, a_dst2, b2, Wu, bu):
        import jax, jax.numpy as jnp
        import numpy as np
        N = 1250
        E = 20000
        D = 768
        H1, C1 = (4, 192)
        H2, C2 = (2, 96)
        EPS = 1e-05
        NEG_SLOPE = 0.2

        def layer_norm(x, g, b):
            mu = x.mean(-1, keepdims=True)
            var = ((x - mu) ** 2).mean(-1, keepdims=True)
            return (x - mu) * jax.lax.rsqrt(var + EPS) * g + b

        def gat_conv(x, src, dst, W, a_src, a_dst, bias, H, C, n):
            h = (x @ W).reshape(n, H, C)
            s_src = (h * a_src).sum(-1)
            s_dst = (h * a_dst).sum(-1)
            e = jax.nn.leaky_relu(s_src[src] + s_dst[dst], NEG_SLOPE)
            emax = jax.ops.segment_max(e, dst, num_segments=n)
            ee = jnp.exp(e - emax[dst])
            denom = jax.ops.segment_sum(ee, dst, num_segments=n)
            alpha = ee / denom[dst]
            out = jax.ops.segment_sum(alpha[:, :, None] * h[src], dst, num_segments=n)
            return out.reshape(n, H * C) + bias
        loops = jnp.arange(N, dtype=edge_index.dtype)
        src = jnp.concatenate([edge_index[0], loops])
        dst = jnp.concatenate([edge_index[1], loops])
        x_norm = layer_norm(x, norm_g, norm_b)
        out1 = gat_conv(x_norm, src, dst, W1, a_src1, a_dst1, b1, H1, C1, N)
        out2 = gat_conv(out1, src, dst, W2, a_src2, a_dst2, b2, H2, C2, N)
        combined = jnp.concatenate([x, out2], axis=-1)
        return combined @ Wu + bu

    def _L1_gnn_ref(x, edge_index, edge_type, W1, q1, k1, b1, W2, q2, k2, b2):
        import jax, jax.numpy as jnp
        import numpy as np
        NEG_SLOPE = 0.2
        EPS = 1e-16
        N_NODES = 4096
        N_EDGES = 20000
        DIM = 768
        HEADS1 = 4
        OUT1 = DIM // HEADS1
        HEADS2 = 1
        OUT2 = DIM
        N_REL = 3

        def rgat_conv(x, W, q, k, b, src, dst, etype, heads, out_ch, n_nodes):
            xr = jnp.einsum('nd,rdf->rnf', x, W)
            oi = xr[etype, dst]
            oj = xr[etype, src]
            qi = oi @ q
            kj = oj @ k
            alpha = jax.nn.leaky_relu(qi + kj, NEG_SLOPE)
            m = jax.ops.segment_max(alpha, dst, num_segments=n_nodes)
            e = jnp.exp(alpha - m[dst])
            z = jax.ops.segment_sum(e, dst, num_segments=n_nodes)
            a = e / (z[dst] + EPS)
            msg = (a[:, :, None] * oj.reshape(-1, heads, out_ch)).reshape(-1, heads * out_ch)
            out = jax.ops.segment_sum(msg, dst, num_segments=n_nodes)
            return out + b
        src, dst = (edge_index[0], edge_index[1])
        n = x.shape[0]
        h = rgat_conv(x, W1, q1, k1, b1, src, dst, edge_type, HEADS1, OUT1, n)
        h = jax.nn.elu(h)
        out = rgat_conv(h, W2, q2, k2, b2, src, dst, edge_type, HEADS2, OUT2, n)
        return out
    edge_index = jnp.stack([src, dst])
    x = _layernorm(x + _L0_gnn_ref(x, edge_index, L0_gnn_norm_g, L0_gnn_norm_b, L0_gnn_W1, L0_gnn_a_src1, L0_gnn_a_dst1, L0_gnn_b1, L0_gnn_W2, L0_gnn_a_src2, L0_gnn_a_dst2, L0_gnn_b2, L0_gnn_Wu, L0_gnn_bu), axis=-1)
    x = _layernorm(x + _L1_gnn_ref(x, edge_index, edge_type_3, L1_gnn_W1, L1_gnn_q1, L1_gnn_k1, L1_gnn_b1, L1_gnn_W2, L1_gnn_q2, L1_gnn_k2, L1_gnn_b2), axis=-1)
    return x

_drawn_inputs = setup_inputs


def setup_inputs(seed=0):
    import zlib

    import numpy as np

    out = dict(_drawn_inputs(seed))
    spreads = {'L0_gnn_norm_g': (1.0, 0.6),
     'L0_gnn_norm_b': (0.0, 0.1),
     'L0_gnn_b1': (0.0, 0.1),
     'L0_gnn_b2': (0.0, 0.1),
     'L0_gnn_bu': (0.0, 0.1),
     'L1_gnn_b1': (0.0, 0.1),
     'L1_gnn_b2': (0.0, 0.1)}
    factors = {'L0_gnn_a_src1': 5.578,
     'L0_gnn_a_dst1': 8.0,
     'L0_gnn_a_src2': 8.0,
     'L0_gnn_a_dst2': 8.0,
     'L1_gnn_W1': 3.914,
     'L1_gnn_q1': 8.0,
     'L1_gnn_k1': 8.0,
     'L1_gnn_q2': 8.0,
     'L1_gnn_k2': 8.0}
    for name, (base, spread) in spreads.items():
        noise = np.random.default_rng([zlib.crc32(name.encode()), seed]).standard_normal(out[name].shape)
        drawn = base * np.exp(spread * noise) if base else spread * noise
        out[name] = jnp.asarray(drawn.astype(out[name].dtype))
    for name, factor in factors.items():
        out[name] = (out[name] * factor).astype(out[name].dtype)
    return out
```

```python
from contextlib import ExitStack, contextmanager

import numpy as np

import concourse.bass as bass
from concourse import mybir

F32 = mybir.dt.float32
F16 = mybir.dt.float16
BF16 = mybir.dt.bfloat16
I32 = mybir.dt.int32
U16 = mybir.dt.uint16
ALU = mybir.AluOpType
ACT = mybir.ActivationFunctionType
AX = mybir.AxisListType

P = 128
N = 1250
D = 768
T = (N + P - 1) // P
NP = T * P
LAST = N - (T - 1) * P
DT = D // P
NE = 40000
EC = 125
NCH = NE // EC
W = 16
W_SHIFT = 4
NW = NP // W
WROW = T * 3 * W
WKEY = 512
SRC_SHIFT = 7
TAB_C0 = 96
RELS = 3
TOTAL = RELS
BIG = 1.0e30
EPS_LN = 1e-5
EPS_Z = 1e-16
WCH = 6
OH = 2
BANKS = 4


class Conv:

    def __init__(self, name, rels, heads, width, v_at, unroll, loops, eps, rows_left):
        self.name, self.rels, self.heads, self.width = name, rels, heads, width
        self.R, self.RH = len(rels), len(rels) * heads
        self.F = heads * width
        self.v_at = v_at
        self.unroll = unroll
        self.loops = loops
        self.piece = min(384, self.F)
        self.pieces = [(r, c) for r in range(self.R) for c in range(0, self.F, self.piece)]
        self.eps = eps
        self.s_rows_at = T + 1 if len(self.pieces) > 1 else T
        self.pq_rows_at = len(self.pieces) * T - rows_left

    def columns(self, i):
        return self.piece + (2 * self.RH if i == 0 else 0)


A = Conv("a", [TOTAL], 4, 192, 0, 2, 2, False, 0)
B = Conv("b", [TOTAL], 2, 96, 8, 2, 1, False, 0)
C = Conv("c", [0, 1, 2], 4, 192, 12, 2, 2, True, 4)
DD = Conv("d", [0, 1, 2], 1, 768, 36, 1, 1, True, 8)
CONVS = [A, B, C, DD]
VCOLS = 42
D_GROUPS = [(0, 4), (4, 3), (7, 3)]
RING = 5
MAXG = NW * NCH
STEP_CREDIT = 30


def gnn_program(nc, t_in, out):
    with ExitStack() as ctx:
        def sb(name, shape, dt):
            return ctx.enter_context(nc.sbuf_tensor(name, shape, dt))

        def sem(name):
            return ctx.enter_context(nc.semaphore(name))

        def dram(name, shape, dt):
            return nc.dram_tensor(name, shape, dt, kind="Internal").ap()

        hx_d = dram("hx_d", [RELS * NP, D], F32)
        nomask_d = dram("nomask_d", [4 * NP, NP], BF16)
        srow_d = dram("srow_d", [4 * 12, NP], F32)
        pqrow_d = dram("pqrow_d", [4 * 24, NP], F32)
        x1_d = dram("x1_d", [NP, D], F32)

        counts = sb("counts", [P, 4, T, NP], U16)
        feat = sb("feat", [P, T * D], F32)
        work = sb("work", [P, 16648], F32)
        identf = sb("identf", [P, P], F32)
        identb = sb("identb", [P, P], BF16)
        vtab = sb("vtab", [P, DT, VCOLS], F32)
        sd = sb("sd", [P, T, 24], F32)
        s02 = sb("s02", [P, T, 12], F32)
        mx = sb("mx", [P, T, 12], F32)
        lk = sb("lk", [P, T, 12], F32)
        mm_ = sb("mm_", [P, T, 4], F32)
        pq = sb("pq", [P, T, 24], F32)
        brow = sb("brow", [P, D], F32)
        zc = sb("zc", [P, 16], F32)
        rz = sb("rz", [P, 16], F32)
        stat = sb("stat", [P, T, 2, 6], F32)
        mv = sb("mv", [P, T, 2], F32)
        sdev = sb("sdev", [P, 2, T], F32)
        epsc = sb("epsc", [P, 1], F32)
        winoff = sb("winoff", [P, NW], F32)
        tab = sb("tab", [1, 192], I32)

        ps = ctx.enter_context(nc.psum_tensor("ps", [P, 8 * 512], F32))

        def bank(b, n=512, at=0):
            return ps[:, b * 512 + at:b * 512 + at + n]

        def carve(region, at, n, dt=F32):
            v = region[:, at:at + n]
            return v if dt == F32 else v.bitcast(dt)

        featv = feat[:, :].rearrange("p (t f) -> p t f", t=T)
        xT = carve(work, 0, DT * NP).rearrange("p (j n) -> p j n", j=DT)
        XT_END = DT * NP
        flat_f = [counts[:, i, :, :].rearrange("p t n -> p (t n)").bitcast(F32) for i in range(4)]
        x_tiles = [flat_f[t // 8][:, t % 8 * D:(t % 8 + 1) * D] for t in range(T)]
        grow, nbrow = flat_f[1][:, 2 * D:3 * D], flat_f[1][:, 3 * D:4 * D]
        wt_a, wt_b = flat_f[TOTAL][0:96, 0:8 * D], flat_f[2][0:96, 0:2 * D]
        space = [XT_END]

        def take(n, dt=F32):
            v = carve(work, space[0], n, dt)
            space[0] += n
            return v

        src_i, dst_i, typ_i, win_i, tile_i = (take(NCH, I32) for _ in range(5))
        lof, keyf = take(NCH), take(NCH)
        dstc, winc = (take(3 * EC, I32).rearrange("p (a e) -> p a e", a=3) for _ in range(2))
        cmin, cmax, cid, cidm, cidp = (take(4)[:, 0:3] for _ in range(5))
        iota_w, tmp_w = take(NW), take(NW)
        act_w = take(6 * NW).rearrange("p (s a w) -> p s a w", s=2, a=3)
        bcol = take(8)
        brow_w = take(3 * NW + 8)
        iota_lo, iota_hi = take(P // 2, F16), take(WROW // 2, F16)
        oh_lo = [take(P // 2, BF16) for _ in range(OH * WCH + 1)]
        oh_hi = [take(WROW // 2, BF16) for _ in range(OH * WCH + 1)]
        MH = NP // 2
        nomask_h = [carve(feat, i * T * MH // 2, T * MH // 2, BF16).rearrange("p (k n) -> p k n", k=T) for i in range(2)]
        nm_out = [carve(work, XT_END + i * (NP // 2), NP // 2, BF16) for i in range(3)]
        WTH = DT * (D // 2)
        wt_half = [carve(feat, i * WTH, WTH) for i in range(3)] + \
                  [carve(work, XT_END + 3 * (NP // 2) + i * WTH, WTH) for i in range(3)] * 3
        wt_half = [v.rearrange("p (f d) -> p f d", f=DT) for v in wt_half]
        WT_HALVES = [(c, r, h) for c in (C, DD) for r in range(RELS) for h in range(2)]
        space[0] = max(space[0], XT_END + 3 * (NP // 2) + 3 * WTH)
        qk1 = take(DT * 8).rearrange("p (j c) -> p j c", j=DT)
        qk2 = take(DT * 2).rearrange("p (j c) -> p j c", j=DT)
        al1 = take(16).rearrange("p (j c) -> p j c", j=8)
        al2 = take(4).rearrange("p (j c) -> p j c", j=2)
        assert space[0] <= 16648
        wring = [carve(work, XT_END, DT * 408), carve(work, XT_END + DT * 408, DT * 384)]
        o0 = XT_END + DT * (408 + 384)
        nm_in = [carve(work, o0 + i * (NP // 2), NP // 2, BF16) for i in range(3)]
        o1 = o0 + 3 * (NP // 2)
        stage = [carve(work, o1 + i * 384, 384) for i in range(3)]
        junk = [carve(feat, 5 * NP, NP // 2, BF16), carve(work, o1 + 3 * 384, NP // 2, BF16)]
        wu = carve(work, XT_END, DT * D).rearrange("p (j c) -> p j c", j=DT)
        o2T = carve(work, XT_END + DT * D, 2 * NP).rearrange("p (j n) -> p j n", j=2)
        wu_tail = carve(work, XT_END + DT * D + 2 * NP, 2 * D).rearrange("p (j c) -> p j c", j=2)
        assert o1 + 3 * 384 + NP // 2 <= 16648
        spare = [flat_f[TOTAL][:, i * D:(i + 1) * D] for i in range(8)]
        sbc = carve(feat, 0, 4 * NP).rearrange("p (h n) -> p h n", h=4)
        rows = carve(feat, 4 * NP, NP)
        xe = [carve(work, i * NP, NP) for i in range(RING)]
        pqb = [carve(work, (RING + 2 * i) * NP, 2 * NP).rearrange("p (c n) -> p c n", c=2) for i in range(2)]
        hx_all = carve(work, (RING + 4) * NP, RING * 769).rearrange("p (s c) -> p s c", s=RING)
        assert (RING + 4) * NP + RING * 769 <= 16648

        phase = sem("phase")
        phases = [0]
        s_const, s_in, s_chunkin = sem("s_const"), sem("s_in"), sem("s_chunkin")
        s_dve, s_last = sem("s_dve"), sem("s_last")
        x_in = sem("x_in")
        ln_std, ln_sqrt, ln_done, ln_turned, ln_copied = (sem(f"ln_{n}") for n in "std sqrt done turned copied".split())
        wt_ab_in = sem("wt_ab_in")
        wt_first = sem("wt_first")
        wt_in = [sem(f"wt_in{i}") for i in range(3)]
        v_done = sem("v_done")
        bnd_ready, bnd_turned = sem("bnd_ready"), sem("bnd_turned")
        oh_ready, oh_used, win_saved = sem("oh_ready"), sem("oh_used"), sem("win_saved")
        extra_ready, extra_used = sem("extra_ready"), sem("extra_used")
        nm_ready, nm_turned, nm_copied = sem("nm_ready"), sem("nm_turned"), sem("nm_copied")
        nm_out_s = [sem(f"nm_out_s{i}") for i in range(3)]

        v_in, sd_done, srow_t, srow_c, srow_out = (sem(n) for n in "v_in sd_done srow_t srow_c srow_out".split())
        pq_ready, pq_t, pq_c, pq_out = (sem(n) for n in "pq_ready pq_t pq_c pq_out".split())
        bias_in, ones = sem("bias_in"), sem("ones")

        class Signal:

            def __init__(self, sem_, before):
                self.sem, self.before = sem_, before

            def at(self, n):
                return self.sem, n + self.before

        class Shared:

            def __init__(self, name):
                self.sem, self.total = sem("layers_" + name), 0

            def layer(self, count):
                self.total += count
                return Signal(self.sem, self.total - count)

        shared = {n: Shared(n) for n in "turned xt_done proj_mm proj_ev max_done x_ready exp_done p_ready p_used "
                  "z_done saved s_in".split()}
        rings = {n: [Shared(f"{n}{i}") for i in range(k)]
                 for n, k in (("w_in", 2), ("nm_in", 3), ("hx_out", 3), ("pq_in", 2), ("hx_in", RING))}

        def ring_share(n, i, size):
            return (n - i + size - 1) // size

        class LayerSems:

            def __init__(self, c):
                turned = 0 if c is A else T
                projected = len(c.pieces) * T
                groups = len(D_GROUPS) if c is DD else c.heads
                steps = groups * c.R * T
                self.turned, self.xt_done = shared["turned"].layer(turned), shared["xt_done"].layer(turned)
                self.proj_mm, self.proj_ev = shared["proj_mm"].layer(projected), shared["proj_ev"].layer(projected)
                self.max_done = shared["max_done"].layer(c.RH * T)
                self.x_ready, self.exp_done = shared["x_ready"].layer(steps), shared["exp_done"].layer(steps)
                self.p_ready, self.p_used = shared["p_ready"].layer(steps), shared["p_used"].layer(steps)
                self.z_done = shared["z_done"].layer(0 if c is DD else 2 * c.heads)
                self.saved = shared["saved"].layer(c.heads * T)
                self.s_in = shared["s_in"].layer(16 * c.R)
                self.w_in = [q.layer(16 * ring_share(len(c.pieces), i, 2)) for i, q in enumerate(rings["w_in"])]
                self.nm_in = [q.layer(16 * ring_share(c.R * T, i, 3)) for i, q in enumerate(rings["nm_in"])]
                self.hx_out = [q.layer(16 * ring_share(projected, i, 3)) for i, q in enumerate(rings["hx_out"])]
                self.pq_in = [q.layer(16 * ring_share(groups * c.R, i, 2)) for i, q in enumerate(rings["pq_in"])]
                self.hx_in = [q.layer(16 * steps // RING) for q in rings["hx_in"]]

        sems = {c: LayerSems(c) for c in CONVS}
        y_mm_used = sem("y_mm_used")
        y_in, y_x, y_turned, y_copied, y_mm = (sem(f"y_{n}") for n in "in x turned copied mm".split())
        y_std, y_sqrt, y_done = sem("y_std"), sem("y_sqrt"), sem("y_done")
        y_out = sem("y_out")
        elu_e, elu_done, elu_min = sem("elu_e"), sem("elu_done"), sem("elu_min")
        f_x = [sem(f"f_x{i}") for i in range(2)]
        f_std, f_sqrt, f_done, f_out = sem("f_std"), sem("f_sqrt"), sem("f_done"), sem("f_out")

        def end_phase(eng, k):
            eng.drain().then_inc(phase, 1)
            eng.wait_ge(phase, 5 * (k + 1))

        @contextmanager
        def trips(eng, c):
            if c.loops == 1:
                yield 0
            else:
                with eng.Fori(0, c.loops) as it:
                    yield it

        def sums_at(c, t):
            if c is B:
                return ps[:, (t // 5) * 512 + (t % 5) * 98:(t // 5) * 512 + (t % 5) * 98 + 97]
            return ps[:, (t // 2) * 512 + (t % 2) * 256:(t // 2) * 512 + (t % 2) * 256 + 193]

        def tiles_per_bank(c):
            return 5 if c is B else 2

        block = ctx.enter_context(nc.Block())

        @block.sync
        def _(sp):
            for a, b in ((src_i, "src"), (dst_i, "dst"), (typ_i, "edge_type")):
                sp.dma_start(a[0:EC, :], t_in[b]).then_inc(s_in, 16)
            sp.dma_start(dstc[:, 0:2, :], t_in["dst_rows"][0:2 * P, :].rearrange("(a p) e -> p a e", p=P)).then_inc(s_chunkin, 16)
            sp.dma_start(dstc[0:NCH - 2 * P, 2, :], t_in["dst_rows"][2 * P:NCH, :]).then_inc(s_chunkin, 16)
            sp.dma_start(grow, t_in["norm_g"].partition_broadcast(P)).then_inc(s_in, 16)
            sp.dma_start(nbrow, t_in["norm_b"].partition_broadcast(P)).then_inc(s_in, 16)
            for n, v in (("qk1", qk1), ("qk2", qk2)):
                sp.dma_start(v, t_in[n]).then_inc(s_in, 16)
            for n, v in (("al1", al1), ("al2", al2)):
                sp.dma_start(v[0:96], t_in[n]).then_inc(s_in, 16)
            sp.dma_start(wt_b.rearrange("p (f d) -> p f d", f=2), t_in["wt_b"].rearrange("(f p) d -> p f d", p=96)).then_inc(wt_ab_in, 16)
            for t in range(T):
                rows_n = P if t < T - 1 else LAST
                if t == T - 1:
                    sp.wait_ge(s_last, 1)
                sp.dma_start(x_tiles[t][0:rows_n, :], t_in["x"][t * P:t * P + rows_n, :]).then_inc(x_in, 16)
            end_phase(sp, 0)
            end_phase(sp, 1)

            for n in range(4 * T):
                sp.wait_ge(nm_copied, n + 1)
                row = (n // T + 1) % 4 * T + n % T
                sp.dma_start(nomask_d[row * P:(row + 1) * P, :], nm_out[n % 3]).then_inc(nm_out_s[n % 3], 16)
            for i in range(3):
                sp.wait_ge(nm_out_s[i], 16 * ring_share(4 * T, i, 3))
            end_phase(sp, 2)

            def layer(ci, c, ph):
                s = sems[c]
                def mask_load(n):
                    r, t = n // T, n % T
                    row = (0 if c.rels[r] == TOTAL else c.rels[r] + 1) * NP + t * P
                    sp.dma_start(nm_in[n % 3], nomask_d[row:row + P, :]).then_inc(s.nm_in[n % 3].sem, 16)

                for n in range(3):
                    mask_load(n)
                sp.wait_ge(srow_c, ci + 1)
                sp.dma_start(srow_d[12 * ci:12 * ci + c.RH, :], rows[0:c.RH, :]).then_inc(srow_out, 16)
                sp.wait_ge(srow_out, 16 * (ci + 1))
                for r in range(c.R):
                    if r:
                        sp.wait_ge(*s.max_done.at(r * T * c.heads))
                    sp.dma_start(sbc[:, 0:c.heads, :].rearrange("p h n -> p (h n)"),
                                 srow_d[12 * ci + r * c.heads:12 * ci + (r + 1) * c.heads, :].rearrange("h n -> (h n)")
                                 .partition_broadcast(P)).then_inc(s.s_in.sem, 16)
                    for t in range(T):
                        n = r * T + t
                        if n >= 3:
                            sp.wait_ge(*s.max_done.at((n - 2) * c.heads))
                            mask_load(n)
                sp.wait_ge(pq_c, ci + 1)
                sp.dma_start(pqrow_d[24 * ci:24 * ci + 2 * c.RH, :], rows[0:2 * c.RH, :]).then_inc(pq_out, 16)
                sp.wait_ge(pq_out, 16 * (ci + 1))
                sp.dma_start(brow[:, 0:c.F], t_in["bias_" + c.name].partition_broadcast(P)).then_inc(bias_in, 16)
                end_phase(sp, ph)

                def pq_load(slot, rh, cols, used):
                    sp.wait_ge(*s.x_ready.at(used))
                    lo, n_ = cols
                    sp.dma_start(pqb[slot][:, :, lo:lo + n_], pqrow_d[bass.ds(24 * ci + rh * 2, 2), lo:lo + n_]
                                 .partition_broadcast(P)).then_inc(s.pq_in[slot].sem, 16)

                def hx_load(n, i, r, k, col):
                    sp.wait_ge(*s.p_used.at(n + 1))
                    sp.dma_start(hx_all[:, i % RING, 1:1 + c.width],
                                 hx_d[(r * T + k) * P:(r * T + k + 1) * P, bass.ds(col, c.width)]) \
                        .then_inc(s.hx_in[i % RING].sem, 16)

                if c is not DD:
                    body = c.unroll * c.R
                    with trips(sp, c) as it:
                        for m in range(body):
                            u, r = m // c.R, m % c.R
                            h = it * c.unroll + u
                            pq_load(m % 2, r * c.heads + h, (0, NP), it * (body * T) + (STEP_CREDIT + (m - 1) * T))
                            for k in range(T):
                                i = m * T + k
                                hx_load(it * (body * T) + i, i, r, k, h * c.width)
                else:
                    for g, (t0, nt) in enumerate(D_GROUPS):
                        for r in range(c.R):
                            pq_load((g * 3 + r) % 2, r, (t0 * P, nt * P), STEP_CREDIT + (g * 3 + r - 1) * T)
                            for k in range(T):
                                i = (g * 3 + r) * T + k
                                hx_load(i, i, r, k, 0)

            layer(0, A, 3)
            end_phase(sp, 4)
            layer(1, B, 5)
            end_phase(sp, 6)

            sp.dma_start(xT[:, :, 0:N], t_in["x_t"].rearrange("(j p) n -> p j n", p=P)).then_inc(y_in, 16)
            sp.dma_start(brow[:, :], t_in["bias_u"].partition_broadcast(P)).then_inc(y_in, 16)
            sp.dma_start(wu, t_in["Wu"][0:D, :].rearrange("(j p) c -> p j c", p=P)).then_inc(y_in, 16)
            sp.dma_start(wu_tail[:, 0, :], t_in["Wu"][D:D + P, :]).then_inc(y_in, 16)
            sp.dma_start(wu_tail[0:64, 1, :], t_in["Wu"][D + P:D + 192, :]).then_inc(y_in, 16)

            def x_load(t):
                rn = P if t < T - 1 else LAST
                sp.dma_start(spare[t % 8][0:rn, :], t_in["x"][t * P:t * P + rn, :]).then_inc(y_x, 16)

            for t in range(8):
                x_load(t)
            for t in range(T):
                sp.wait_ge(y_done, t + 1)
                if t < T - 8:
                    x_load(t + 8)
                sp.dma_start(x1_d[t * P:(t + 1) * P, :], featv[:, t, :]).then_inc(y_out, 16)
            sp.wait_ge(y_out, 16 * T)
            end_phase(sp, 7)

            layer(2, C, 8)
            end_phase(sp, 9)
            layer(3, DD, 10)
            end_phase(sp, 11)
            for t in range(T):
                if t >= 2:
                    sp.wait_ge(f_done, t - 1)
                sp.dma_start(xe[0][:, 0:D] if t % 2 == 0 else xe[1][:, 0:D],
                             x1_d[t * P:(t + 1) * P, :]).then_inc(f_x[t % 2], 16)
            for t in range(T):
                rn = P if t < T - 1 else LAST
                sp.wait_ge(f_done, t + 1)
                sp.dma_start(out[t * P:t * P + rn, :], featv[0:rn, t, :]).then_inc(f_out, 16)
            sp.wait_ge(f_out, 16 * T)

        @block.gpsimd
        def _(pool):
            def then(ins):
                pool_n[0] += 1
                ins.then_inc(s_const, 1)
                return pool_n[0]
            pool_n = [0]
            then(nc.gpsimd.memset(identf[:, :], 0.0))
            then(nc.gpsimd.memset(identb[:, :], 0.0))
            pool.wait_ge(s_const, 2)
            then(nc.gpsimd.affine_select(out=identf[:, :], in_=identf[:, :], compare_op=ALU.not_equal, fill=1.0,
                                         base=0, pattern=[[-1, P]], channel_multiplier=1))
            then(nc.gpsimd.affine_select(out=identb[:, :], in_=identb[:, :], compare_op=ALU.not_equal, fill=1.0,
                                         base=0, pattern=[[-1, P]], channel_multiplier=1))
            then(nc.gpsimd.memset(epsc[:, :], EPS_LN))
            imp = dict(allow_small_or_imprecise_dtypes=True)
            then(nc.gpsimd.iota(iota_lo, [[1, P]], base=0, channel_multiplier=0, **imp))
            then(nc.gpsimd.iota(iota_hi, [[1, WROW]], base=0, channel_multiplier=0, **imp))
            then(nc.gpsimd.iota(winoff[:, :], [[WKEY, NW]], base=0, channel_multiplier=0, **imp))
            then(nc.gpsimd.iota(iota_w, [[1, NW]], base=0, channel_multiplier=0, **imp))
            then(nc.gpsimd.iota(cid, [[P, 3]], base=0, channel_multiplier=1, **imp))
            assert pool_n[0] == 10
            end_phase(pool, 0)
            end_phase(pool, 1)

            def wt_load(i):
                c, r, h = WT_HALVES[i]
                pool.dma_start(wt_half[i], t_in["wt_" + c.name][r].rearrange("(f p) d -> p f d", p=P)
                               [:, :, h * (D // 2):(h + 1) * (D // 2)]).then_inc(wt_in[i % 3], 16)

            for i in range(3, 12):
                if i >= 6:
                    pool.wait_ge(v_done, 1 + i - 2)
                wt_load(i)
            for k in range(2, 12):
                end_phase(pool, k)

        @block.tensor
        def _(pe):
            mm = nc.tensor.matmul
            pe.wait_ge(s_const, 10)

            pe.wait_ge(bnd_ready, 1)
            for s_ in range(2):
                for a in range(3):
                    last = nc.tensor.transpose(ps[0:NW, (4 + s_) * 512 + a * P:(4 + s_) * 512 + (a + 1) * P],
                                               act_w[:, s_, a, :], identf[:, :])
            last.then_inc(bnd_turned, 1)
            pe.wait_ge(bnd_ready, 2)
            for i in range(2):
                last = nc.tensor.transpose(ps[0:1, 7 * 512 + i * P:7 * 512 + i * P + NW],
                                           bcol[0:NW, i:i + 1], identf[0:NW, 0:NW])
            last.then_inc(bnd_turned, 1)

            pe.wait_ge(s_in, 16 * 9)
            pe.wait_ge(wt_ab_in, 32)
            for c, wt, al, per, at in ((A, wt_a, al1, 2, 0), (B, wt_b, al2, 1, 48)):
                for j in range(DT):
                    for h in range(c.heads):
                        for q in range(per):
                            f = h * per + q
                            last = mm(bank(6, 2, at + (j * c.heads + h) * 2), wt[:, f * D + j * P:f * D + (j + 1) * P],
                                      al[0:96, f, :], start=(q == 0), stop=(q == per - 1))
            last.then_inc(v_done, 1)
            for t in range(T):
                pe.wait_ge(ln_done, t + 1)
                if t >= 2:
                    pe.wait_ge(ln_copied, t - 1)
                for j in range(DT):
                    last = nc.tensor.transpose(ps[:, t % 2 * 1024 + j * P:t % 2 * 1024 + (j + 1) * P],
                                               x_tiles[t][:, j * P:(j + 1) * P], identf[:, :])
                last.then_inc(ln_turned, 1)
            end_phase(pe, 0)

            pe.sem_inc(oh_used, OH)
            pe.sem_inc(extra_used, 1)

            def edge_product(b, slot, start):
                return mm(bank(b, WROW), oh_lo[slot][0:EC, :], oh_hi[slot][0:EC, :],
                          start=start, stop=False, skip_group_check=True)

            def windows(extra):
                with pe.Fori(0, NW // BANKS) as i:
                    for u in range(BANKS):
                        w = i * BANKS + u
                        pe.wait_ge(win_saved, w + 1)
                        pe.wait_ge(oh_ready, w + 1)
                        for q in range(WCH):
                            last = edge_product(u, u % OH * WCH + q, q == 0)
                        last.then_inc(oh_used, 1)
                        if extra:
                            e0 = pe.value_load(tab[0:1, bass.ds(w, 1)], min_val=0, max_val=MAXG)
                            e1 = pe.value_load(tab[0:1, bass.ds(w + 1, 1)], min_val=0, max_val=MAXG)
                            with pe.If(e0 < e1):
                                with pe.Fori(e0, e1) as e:
                                    pe.wait_ge(extra_ready, e + 1)
                                    edge_product(u, OH * WCH, False).then_inc(extra_used, 1)

            extras = pe.value_load(tab[0:1, NW:NW + 1], min_val=0, max_val=MAXG)
            with pe.If(extras < 1):
                windows(False)
            with pe.Else():
                windows(True)
            end_phase(pe, 1)

            def score_weights(i):
                c, r, h = WT_HALVES[i]
                if i < 3:
                    pe.wait_ge(wt_first, 48)
                else:
                    pe.wait_ge(wt_in[i % 3], 16 * (i // 3))
                qk = qk1 if c is C else qk2
                n2 = 2 * c.heads
                for j in range(DT // 2):
                    for f in range(DT):
                        last = mm(bank(6, n2, i * 24 + j * n2), wt_half[i][:, f, j * P:(j + 1) * P],
                                  qk[:, f, :], start=(f == 0), stop=(f == DT - 1))
                last.then_inc(v_done, 1)

            for i in range(3):
                score_weights(i)
            for q in range(8):
                pe.wait_ge(nm_ready, q + 1)
                for t in range(T // 2):
                    n = q * (T // 2) + t
                    if n >= 3:
                        pe.wait_ge(nm_copied, n - 2)
                    o = ps[:, (n % 3) * 1024:(n % 3) * 1024 + NP // 2].bitcast(BF16)
                    for k in range(T):
                        last = nc.tensor.transpose(o[:, k * P:(k + 1) * P], nomask_h[q % 2][:, k, t * P:(t + 1) * P],
                                                   identb[:, :])
                    last.then_inc(nm_turned, 1)
                score_weights(3 + q)
            score_weights(11)
            end_phase(pe, 2)

            def layer(ci, c, ph, turn):
                s = sems[c]
                if turn:
                    for t in range(T):
                        if t >= 2:
                            pe.wait_ge(*s.xt_done.at(t - 1))
                        if c is DD:
                            pe.wait_ge(elu_done, t + 1)
                        for j in range(DT):
                            last = nc.tensor.transpose(ps[:, (t % 2) * 1024 + j * P:(t % 2) * 1024 + (j + 1) * P],
                                                       featv[:, t, j * P:(j + 1) * P], identf[:, :])
                        last.then_inc(s.turned.sem, 1)
                    pe.wait_ge(*s.xt_done.at(T))
                def turn_rows(ready, columns, number, turned_rows):
                    pe.wait_ge(ready, ci + 1)
                    for t in range(T):
                        last = nc.tensor.transpose(ps[0:number, 5 * 512 + t * P:5 * 512 + (t + 1) * P],
                                                   columns[:, t, 0:number], identf[:, :])
                    last.then_inc(turned_rows, 1)

                n = 0
                for i, (r, cc) in enumerate(c.pieces):
                    pe.wait_ge(*s.w_in[i % 2].at(16 * (i // 2 + 1)))
                    if i == 0:
                        pe.wait_ge(v_in, ci + 1)
                    cols = c.columns(i)
                    wv = wring[i % 2][:, 0:DT * cols].rearrange("p (j c) -> p j c", j=DT)
                    for t in range(T):
                        if n == c.s_rows_at:
                            turn_rows(sd_done, sd, c.RH, srow_t)
                        if n == c.pq_rows_at:
                            turn_rows(pq_ready, pq, 2 * c.RH, pq_t)
                        if n >= 4:
                            pe.wait_ge(*s.proj_ev.at(n - 3))
                        for j in range(DT):
                            last = mm(bank(n % 4, cols), xT[:, j, t * P:(t + 1) * P], wv[:, j, :],
                                      start=(j == 0), stop=(j == DT - 1))
                        last.then_inc(s.proj_mm.sem, 1)
                        n += 1
                if n == c.s_rows_at:
                    turn_rows(sd_done, sd, c.RH, srow_t)
                if n == c.pq_rows_at:
                    turn_rows(pq_ready, pq, 2 * c.RH, pq_t)
                end_phase(pe, ph)
                if c is A:
                    pe.sem_inc(s.p_used.sem, RING)
                pe.wait_ge(ones, ci + 1)
                if c is not DD:
                    body = c.unroll * c.R
                    tb = tiles_per_bank(c)
                    with trips(pe, c) as it:
                        for i in range(body * T):
                            m, k = i // T, i % T
                            u, r = m // c.R, m % c.R
                            n = it * (body * T) + i
                            pe.wait_ge(*s.p_ready.at(n + 1))
                            pe.wait_ge(*s.hx_in[i % RING].at(it * (16 * body * T // RING) + 16 * (i // RING + 1)))
                            for t in range(T):
                                if r == 0 and k == 0 and t % tb == 0:
                                    pe.wait_ge(*s.saved.at((it * c.unroll + u) * T + (t + tb)))
                                last = mm(sums_at(c, t), xe[i % RING][:, t * P:(t + 1) * P],
                                          hx_all[:, i % RING, 0:1 + c.width],
                                          start=(r == 0 and k == 0 and t % tb == 0), stop=(r == c.R - 1 and k == T - 1),
                                          skip_group_check=True)
                            last.then_inc(s.p_used.sem, 1)
                else:
                    for g, (t0, nt) in enumerate(D_GROUPS):
                        for r in range(c.R):
                            for k in range(T):
                                i = (g * 3 + r) * T + k
                                pe.wait_ge(*s.p_ready.at(i + 1))
                                pe.wait_ge(*s.hx_in[i % RING].at(16 * (i // RING + 1)))
                                for q in range(nt):
                                    if r == 0 and k == 0 and g:
                                        pe.wait_ge(*s.saved.at(T + D_GROUPS[g - 1][0] + q + 1))
                                    for v, (a, b) in enumerate(((0, 385), (385, 769))):
                                        last = mm(bank(2 * q + v, b - a), xe[i % RING][:, q * P:(q + 1) * P],
                                                  hx_all[:, i % RING, a:b],
                                                  start=(r == 0 and k == 0), stop=(r == c.R - 1 and k == T - 1))
                                last.then_inc(s.p_used.sem, 1)

            layer(0, A, 3, False)
            end_phase(pe, 4)
            layer(1, B, 5, True)
            end_phase(pe, 6)

            for t in range(T):
                if t >= 2:
                    pe.wait_ge(y_copied, t - 1)
                for j, n_ in ((0, P), (1, 64)):
                    last = nc.tensor.transpose(ps[0:n_, (6 + t % 2) * 512 + j * P:(6 + t % 2) * 512 + (j + 1) * P],
                                               featv[:, t, j * P:j * P + n_], identf[:, :])
                last.then_inc(y_turned, 1)
            pe.wait_ge(y_copied, T)
            pe.wait_ge(y_in, 16 * 5)
            for t in range(T):
                if t >= 3:
                    pe.wait_ge(y_mm_used, t - 2)
                for q in range(2):
                    o = bank(2 * (t % 3) + q, 384)
                    cols = slice(q * 384, (q + 1) * 384)
                    for j in range(DT):
                        mm(o, xT[:, j, t * P:(t + 1) * P], wu[:, j, cols], start=(j == 0), stop=False)
                    mm(o, o2T[:, 0, t * P:(t + 1) * P], wu_tail[:, 0, cols], start=False, stop=False)
                    last = mm(o, o2T[0:64, 1, t * P:(t + 1) * P], wu_tail[0:64, 1, cols], start=False, stop=True)
                last.then_inc(y_mm, 1)
            end_phase(pe, 7)

            layer(2, C, 8, True)
            end_phase(pe, 9)
            layer(3, DD, 10, True)
            end_phase(pe, 11)

        @block.scalar
        def _(act):
            act.dma_start(wt_a.rearrange("p (f d) -> p f d", f=8), t_in["wt_a"].rearrange("(f p) d -> p f d", p=96)).then_inc(wt_ab_in, 16)
            for i in range(3):
                c, r, h = WT_HALVES[i]
                act.dma_start(wt_half[i], t_in["wt_" + c.name][r].rearrange("(f p) d -> p f d", p=P)
                              [:, :, h * (D // 2):(h + 1) * (D // 2)]).then_inc(wt_first, 16)
            act.wait_ge(s_const, 10)
            act.wait_ge(ln_std, 1)
            nc.scalar.activation(sdev[:, 0, :], mv[:, :, 1], ACT.Sqrt, bias=epsc[:, 0:1]).then_inc(ln_sqrt, 1)
            for t in range(T):
                act.wait_ge(ln_turned, t + 1)
                nc.scalar.activation(xT[:, :, t * P:(t + 1) * P],
                                     ps[:, t % 2 * 1024:t % 2 * 1024 + D].rearrange("p (j n) -> p j n", j=DT),
                                     ACT.Copy).then_inc(ln_copied, 1)
            end_phase(act, 0)

            act.sem_inc(win_saved, BANKS)
            def windows(extra):
                with act.Fori(0, NW // BANKS) as i:
                    for u in range(BANKS):
                        w = i * BANKS + u
                        act.wait_ge(oh_used, w + (OH + 1))
                        if extra:
                            e1 = act.value_load(tab[0:1, bass.ds(w + 1, 1)], min_val=0, max_val=MAXG)
                            act.wait_ge(extra_used, e1 + 1)
                        sums = bank(u, WROW).rearrange("p (k r x) -> p r k x", k=T, r=3)
                        for r in range(3):
                            last = nc.scalar.activation(counts[:, r, :, bass.ds(w * W, W)], sums[:, r], ACT.Copy)
                        last.then_inc(win_saved, 1)

            extras = act.value_load(tab[0:1, NW:NW + 1], min_val=0, max_val=MAXG)
            with act.If(extras < 1):
                windows(False)
            with act.Else():
                windows(True)
            end_phase(act, 1)

            for n in range(4 * T):
                act.wait_ge(nm_turned, n + 1)
                if n >= 3:
                    act.wait_ge(nm_out_s[n % 3], 16 * (n // 3))
                o = ps[:, (n % 3) * 1024:(n % 3) * 1024 + NP // 2].bitcast(BF16)
                nc.scalar.activation(nm_out[n % 3], o, ACT.Copy).then_inc(nm_copied, 1)
            end_phase(act, 2)

            def layer(ci, c, ph, turn, shift):
                s = sems[c]
                def w_load(i):
                    r, cc = c.pieces[i]
                    src = t_in["w_" + c.name]
                    act.dma_start(wring[i % 2][:, 0:DT * c.columns(i)].rearrange("p (j c) -> p j c", j=DT)[:, :, 0:c.piece],
                                  src[r * D:(r + 1) * D, cc:cc + c.piece].rearrange("(j p) c -> p j c", p=P)) \
                        .then_inc(s.w_in[i % 2].sem, 16)

                w_load(0)
                if len(c.pieces) > 1:
                    w_load(1)
                def elu_exp(t):
                    act.wait_ge(elu_min, t + 1)
                    nc.scalar.activation(spare[t % 8], spare[t % 8], ACT.Exp).then_inc(elu_e, 1)

                if c is DD:
                    elu_exp(0)
                    elu_exp(1)
                if turn:
                    for t in range(T):
                        if c is DD and t + 2 < T:
                            elu_exp(t + 2)
                        act.wait_ge(*s.turned.at(t + 1))
                        nc.scalar.activation(xT[:, :, t * P:(t + 1) * P],
                                             ps[:, (t % 2) * 1024:(t % 2) * 1024 + D].rearrange("p (j n) -> p j n", j=DT),
                                             ACT.Copy, bias=shift).then_inc(s.xt_done.sem, 1)
                def copy_rows(turned_rows, number, copied):
                    act.wait_ge(turned_rows, ci + 1)
                    nc.scalar.activation(rows[0:number, :], ps[0:number, 5 * 512:5 * 512 + NP], ACT.Copy).then_inc(copied, 1)

                n = 0
                for i, (r, cc) in enumerate(c.pieces):
                    for t in range(T):
                        if n == c.s_rows_at:
                            copy_rows(srow_t, c.RH, srow_c)
                        if n == c.pq_rows_at:
                            copy_rows(pq_t, 2 * c.RH, pq_c)
                        act.wait_ge(*s.proj_mm.at(n + 1))
                        if n >= 3:
                            act.wait_ge(*s.hx_out[n % 3].at(16 * (n // 3)))
                        if i == 0:
                            sums = bank(n % 4, 2 * c.RH, c.piece)
                            nc.scalar.activation(s02[:, t, 0:c.RH], sums[:, 0:c.RH], ACT.Copy, scale=0.2)
                            last = nc.scalar.activation(sd[:, t, 0:2 * c.RH], sums, ACT.Copy)
                            if t == T - 1:
                                last.then_inc(sd_done, 1)
                        nc.scalar.activation(stage[n % 3][:, 0:c.piece], bank(n % 4, c.piece), ACT.Copy).then_inc(s.proj_ev.sem, 1)
                        act.wait_ge(*s.proj_ev.at(n + 1))
                        act.dma_start(hx_d[(r * T + t) * P:(r * T + t + 1) * P, cc:cc + c.piece],
                                      stage[n % 3][:, 0:c.piece]).then_inc(s.hx_out[n % 3].sem, 16)
                        n += 1
                    if i + 2 < len(c.pieces):
                        w_load(i + 2)
                if n == c.s_rows_at:
                    copy_rows(srow_t, c.RH, srow_c)
                if n == c.pq_rows_at:
                    copy_rows(pq_t, 2 * c.RH, pq_c)
                for q in range(3):
                    act.wait_ge(*s.hx_out[q].at(16 * ((n - q + 2) // 3)))
                end_phase(act, ph)

                def exp(n, i, k, rh, n_):
                    act.wait_ge(*s.x_ready.at(n + STEP_CREDIT + 1))
                    nc.scalar.activation(xe[i % RING][:, 0:n_], xe[i % RING][:, 0:n_], ACT.Exp,
                                         bias=s02[:, k, bass.ds(rh, 1)], scale=0.8).then_inc(s.exp_done.sem, 1)

                if c is not DD:
                    body = c.unroll * c.R
                    with trips(act, c) as it:
                        for i in range(body * T):
                            m, k = i // T, i % T
                            u, r = m // c.R, m % c.R
                            exp(it * (body * T) + i, i, k, r * c.heads + it * c.unroll + u, NP)
                else:
                    for g, (t0, nt) in enumerate(D_GROUPS):
                        for r in range(c.R):
                            for k in range(T):
                                i = (g * 3 + r) * T + k
                                exp(i, i, k, r, nt * P)

            layer(0, A, 3, False, 0.0)
            end_phase(act, 4)
            layer(1, B, 5, True, 0.0)
            end_phase(act, 6)

            for t in range(T):
                act.wait_ge(y_turned, t + 1)
                nc.scalar.activation(o2T[:, 0, t * P:(t + 1) * P], ps[:, (6 + t % 2) * 512:(6 + t % 2) * 512 + P], ACT.Copy)
                nc.scalar.activation(o2T[0:64, 1, t * P:(t + 1) * P],
                                     ps[0:64, (6 + t % 2) * 512 + P:(6 + t % 2) * 512 + 2 * P], ACT.Copy).then_inc(y_copied, 1)
            for t in range(T):
                act.wait_ge(y_std, t + 1)
                nc.scalar.activation(sdev[:, 0, t:t + 1], mv[:, t, 1:2], ACT.Sqrt, bias=epsc[:, 0:1]).then_inc(y_sqrt, 1)
            end_phase(act, 7)

            layer(2, C, 8, True, 0.0)
            end_phase(act, 9)
            layer(3, DD, 10, True, -1.0)
            end_phase(act, 11)
            for t in range(T):
                act.wait_ge(f_std, t + 1)
                nc.scalar.activation(sdev[:, 0, t:t + 1], mv[:, t, 1:2], ACT.Sqrt, bias=epsc[:, 0:1]).then_inc(f_sqrt, 1)

        @block.vector
        def _(dve):
            v = nc.vector
            n_link = [0]

            def link(ins):
                n_link[0] += 1
                ins.then_inc(s_dve, 1)
                dve.wait_ge(s_dve, n_link[0])

            def norm_stats(x, t, std):
                for q in range(2):
                    st = v.bn_stats(stat[:, t, q, :], x[:, q * 384:(q + 1) * 384])
                link(st)
                ins = v.bn_aggr(mv[:, t, :], stat[:, t, :, :].rearrange("p a b -> p (a b)"))
                if std is not None:
                    ins.then_inc(std, 1)
                return ins

            def norm_apply(o, x, t):
                link(v.reciprocal(sdev[:, 1, t:t + 1], sdev[:, 0, t:t + 1]))
                return v.tensor_scalar(o, x, mv[:, t, 0:1], sdev[:, 1, t:t + 1], ALU.subtract, ALU.mult)

            v.memset(x_tiles[T - 1], 0.0).then_inc(s_last, 1)
            v.memset(cmin, 1.0e4)
            link(v.memset(cmax, -1.0))
            dve.wait_ge(s_const, 10)
            dve.wait_ge(s_chunkin, 32)
            tail = NCH - 2 * P
            v.tensor_scalar(winc[:, 0:2, :], dstc[:, 0:2, :], W_SHIFT, None, ALU.logical_shift_right)
            link(v.tensor_scalar(winc[0:tail, 2, :], dstc[0:tail, 2, :], W_SHIFT, None, ALU.logical_shift_right))
            v.tensor_reduce(cmin[:, 0:2], winc[:, 0:2, :], AX.X, ALU.min)
            v.tensor_reduce(cmin[0:tail, 2:3], winc[0:tail, 2, :], AX.X, ALU.min)
            v.tensor_reduce(cmax[:, 0:2], winc[:, 0:2, :], AX.X, ALU.max)
            v.tensor_reduce(cmax[0:tail, 2:3], winc[0:tail, 2, :], AX.X, ALU.max)
            v.tensor_scalar(cidm, cid, -1000.0, None, ALU.add)
            link(v.tensor_scalar(cidp, cid, 1.0, None, ALU.add))
            for a in range(3):
                link(v.tensor_scalar(tmp_w, iota_w, cmin[:, a:a + 1], None, ALU.is_ge))
                link(v.scalar_tensor_tensor(tmp_w, iota_w, cmax[:, a:a + 1], tmp_w, ALU.is_le, ALU.mult))
                v.tensor_scalar(act_w[:, 0, a, :], tmp_w, cidm[:, a:a + 1], 1000.0, ALU.mult, ALU.add)
                link(v.tensor_scalar(act_w[:, 1, a, :], tmp_w, cidp[:, a:a + 1], None, ALU.mult))
            v.nop().then_inc(bnd_ready, 1)
            dve.wait_ge(bnd_turned, 1)
            v.tensor_reduce(bcol[0:NW, 2:3], ps[0:NW, 4 * 512:4 * 512 + 3 * P], AX.X, ALU.min)
            link(v.tensor_reduce(bcol[0:NW, 3:4], ps[0:NW, 5 * 512:5 * 512 + 3 * P], AX.X, ALU.max))
            link(v.tensor_scalar(bcol[0:NW, 0:1], bcol[0:NW, 2:3], float(NCH - WCH), None, ALU.min))
            link(v.tensor_scalar(bcol[0:NW, 4:5], bcol[0:NW, 0:1], float(WCH), None, ALU.add))
            link(v.tensor_tensor(bcol[0:NW, 5:6], bcol[0:NW, 4:5], bcol[0:NW, 3:4], ALU.max))
            link(v.tensor_tensor(bcol[0:NW, 1:2], bcol[0:NW, 5:6], bcol[0:NW, 4:5], ALU.subtract))
            v.nop().then_inc(bnd_ready, 1)
            dve.wait_ge(bnd_turned, 2)
            lo, num, cum = brow_w[0:1, 0:NW], brow_w[0:1, NW:2 * NW], brow_w[0:1, 2 * NW:3 * NW + 1]
            v.memset(cum, 0.0)
            v.tensor_copy(lo, ps[0:1, 7 * 512:7 * 512 + NW])
            link(v.tensor_copy(num, ps[0:1, 7 * 512 + P:7 * 512 + P + NW]))
            link(v.tensor_tensor_scan(cum[:, 1:NW + 1], num, num, 0.0, ALU.add, ALU.max))
            v.tensor_copy(tab[:, 0:NW + 1], cum)
            v.tensor_copy(tab[:, TAB_C0:TAB_C0 + NW], lo)
            dve.wait_ge(s_in, 16 * 9)
            v.tensor_scalar(win_i[0:EC, :], dst_i[0:EC, :], W_SHIFT, None, ALU.logical_shift_right)
            link(v.tensor_scalar(tile_i[0:EC, :], src_i[0:EC, :], SRC_SHIFT, None, ALU.logical_shift_right))
            link(v.scalar_tensor_tensor(keyf[0:EC, :], win_i[0:EC, :], float(WKEY - W), dst_i[0:EC, :], ALU.mult, ALU.add))
            link(v.scalar_tensor_tensor(keyf[0:EC, :], typ_i[0:EC, :], float(W), keyf[0:EC, :], ALU.mult, ALU.add))
            link(v.scalar_tensor_tensor(keyf[0:EC, :], tile_i[0:EC, :], float(3 * W), keyf[0:EC, :], ALU.mult, ALU.add))
            v.scalar_tensor_tensor(lof[0:EC, :], tile_i[0:EC, :], -float(P), src_i[0:EC, :], ALU.mult, ALU.add)

            dve.wait_ge(s_last, 1)
            for t in range(T):
                dve.wait_ge(x_in, 16 * T)
                last = norm_stats(x_tiles[t], t, ln_std if t == T - 1 else None)
            dve.wait_ge(ln_sqrt, 1)
            link(v.reciprocal(sdev[:, 1, :], sdev[:, 0, :]))
            for t in range(T):
                x = x_tiles[t]
                link(v.scalar_tensor_tensor(x, x, mv[:, t, 0:1], grow, ALU.subtract, ALU.mult))
                v.scalar_tensor_tensor(x, x, sdev[:, 1, t:t + 1], nbrow, ALU.mult, ALU.add).then_inc(ln_done, 1)
            dve.wait_ge(v_done, 1)
            for c, at in ((A, 0), (B, 48)):
                for q in range(2):
                    v.tensor_copy(vtab[:, :, c.v_at + q * c.heads:c.v_at + (q + 1) * c.heads],
                                  bank(6, DT * 2 * c.heads, at).rearrange("p (j h q) -> p j h q", j=DT, q=2)[:, :, :, q])
            end_phase(dve, 0)

            def one_hot_lo(slot, ch):
                return v.tensor_scalar(oh_lo[slot][0:EC, :], iota_lo[0:EC, :], lof[0:EC, bass.ds(ch, 1)],
                                         None, ALU.is_equal)

            def one_hot_hi(slot, w, ch):
                return v.tensor_scalar(oh_hi[slot][0:EC, :], iota_hi[0:EC, :], winoff[0:EC, bass.ds(w, 1)],
                                       keyf[0:EC, bass.ds(ch, 1)], ALU.add, ALU.is_equal)

            def windows(extra):
                with dve.Fori(0, NW // BANKS) as i:
                    for u in range(BANKS):
                        w = i * BANKS + u
                        c0 = dve.value_load(tab[0:1, bass.ds(w + TAB_C0, 1)], min_val=0, max_val=NCH - WCH)
                        dve.wait_ge(oh_used, w + 1)
                        for q in range(WCH):
                            one_hot_lo(u % OH * WCH + q, c0 + q)
                        for q in range(WCH):
                            last = one_hot_hi(u % OH * WCH + q, w, c0 + q)
                        last.then_inc(oh_ready, 1)
                        if extra:
                            e0 = dve.value_load(tab[0:1, bass.ds(w, 1)], min_val=0, max_val=MAXG)
                            e1 = dve.value_load(tab[0:1, bass.ds(w + 1, 1)], min_val=0, max_val=MAXG)
                            with dve.If(e0 < e1):
                                with dve.Fori(e0, e1) as e:
                                    ch = nc.s_assert_within(
                                        e - e0 + c0 + WCH, 0, NCH - 1, skip_runtime_bounds_check_because=
                                        "a window's chunks end with the last chunk at most")
                                    dve.wait_ge(extra_used, e + 1)
                                    one_hot_lo(OH * WCH, ch)
                                    one_hot_hi(OH * WCH, w, ch).then_inc(extra_ready, 1)

            extras = dve.value_load(tab[0:1, NW:NW + 1], min_val=0, max_val=MAXG)
            with dve.If(extras < 1):
                windows(False)
            with dve.Else():
                windows(True)
            end_phase(dve, 1)

            flat = [counts[:, x, :, :].rearrange("p k n -> p (k n)") for x in range(4)]
            link(v.tensor_tensor(flat[TOTAL], flat[0], flat[1], ALU.add))
            link(v.tensor_tensor(flat[TOTAL], flat[TOTAL], flat[2], ALU.add))
            for k in range(T):
                o = counts[:, TOTAL, k, k * P:(k + 1) * P]
                last = v.tensor_tensor(o, o, identb[:, :], ALU.add)
            link(last)
            dve.wait_ge(v_done, 1 + 3)
            for q in range(8):
                if q >= 2:
                    dve.wait_ge(nm_turned, (q - 1) * (T // 2))
                v.tensor_scalar(nomask_h[q % 2], counts[:, q // 2, :, q % 2 * MH:(q % 2 + 1) * MH], 0.0, BIG,
                                ALU.is_equal, ALU.mult).then_inc(nm_ready, 1)
            dve.wait_ge(v_done, 1 + 12)
            for i, (c, r, h) in enumerate(WT_HALVES):
                for q in range(2):
                    at = c.v_at + q * c.RH + r * c.heads
                    v.tensor_copy(vtab[:, h * (DT // 2):(h + 1) * (DT // 2), at:at + c.heads],
                                  bank(6, 3 * 2 * c.heads, i * 24).rearrange("p (j q h) -> p j q h", j=DT // 2, q=2)[:, :, q, :])
            end_phase(dve, 2)

            def elu():
                def low(t):
                    if t >= 8:
                        dve.wait_ge(elu_done, t - 7)
                    v.tensor_scalar(spare[t % 8], featv[:, t, :], 0.0, None, ALU.min).then_inc(elu_min, 1)
                low(0)
                low(1)
                for t in range(T):
                    dve.wait_ge(elu_e, t + 1)
                    v.scalar_tensor_tensor(featv[:, t, :], featv[:, t, :], 0.0, spare[t % 8], ALU.max,
                                           ALU.add).then_inc(elu_done, 1)
                    if t + 2 < T:
                        low(t + 2)

            def layer(ci, c, ph):
                s = sems[c]
                H, R, RH = c.heads, c.R, c.RH
                v.tensor_copy(wring[0][:, 0:DT * c.columns(0)].rearrange("p (j c) -> p j c", j=DT)[:, :, c.piece:],
                              vtab[:, :, c.v_at:c.v_at + 2 * RH]).then_inc(v_in, 1)
                if c is DD:
                    elu()
                n = 0
                for r in range(R):
                    dve.wait_ge(*s.s_in.at(16 * (r + 1)))
                    for t in range(T):
                        dve.wait_ge(*s.nm_in[n % 3].at(16 * (n // 3 + 1)))
                        for h in range(H):
                            if n * H + h >= 2:
                                dve.wait_ge(*s.max_done.at(n * H + h - 1))
                            v.tensor_tensor_reduce(junk[(n * H + h) % 2], sbc[:, h, :], nm_in[n % 3], 1.0, -3.0e38,
                                                          ALU.subtract, ALU.max, mx[:, t, r * H + h:r * H + h + 1]) \
                                .then_inc(s.max_done.sem, 1)
                        n += 1
                dve.wait_ge(*s.max_done.at(R * T * H))
                d_ = sd[:, :, RH:2 * RH]
                lv = lk[:, :, 0:RH]
                link(v.tensor_tensor(lv, mx[:, :, 0:RH], d_, ALU.add))
                link(v.scalar_tensor_tensor(lv, lv, 0.2, lv, ALU.mult, ALU.max))
                m = lk[:, :, 0:H]
                for r in range(1, R):
                    link(v.tensor_tensor(mm_[:, :, 0:H], m, lk[:, :, r * H:(r + 1) * H], ALU.max))
                    m = mm_[:, :, 0:H]
                link(v.scalar_tensor_tensor(mx[:, :, 0:H], m, -0.1 * BIG, m, ALU.is_gt, ALU.mult))
                link(v.tensor_scalar(mx[:, :, 0:H], mx[:, :, 0:H], -1.25, None, ALU.mult))
                pqv = pq[:, :, 0:2 * RH].rearrange("p t (c k) -> p t c k", k=2)
                for r in range(R):
                    last = v.scalar_tensor_tensor(pqv[:, :, r * H:(r + 1) * H, 1], sd[:, :, RH + r * H:RH + (r + 1) * H],
                                                  0.25, mx[:, :, 0:H], ALU.mult, ALU.add)
                link(last)
                v.tensor_tensor(pqv[:, :, :, 0], pqv[:, :, :, 1], d_, ALU.add).then_inc(pq_ready, 1)
                end_phase(dve, ph)

                if c is A:
                    dve.sem_inc(s.x_ready.sem, STEP_CREDIT)
                    dve.sem_inc(s.saved.sem, T)
                v.memset(hx_all[:, :, 0:1], 1.0).then_inc(ones, 1)
                dve.wait_ge(bias_in, 16 * (ci + 1))

                def exponents(n, i, k, rh, slot, uses, lo, n_):
                    dve.wait_ge(*s.p_used.at(n + 1))
                    if k == 0:
                        dve.wait_ge(*s.pq_in[slot].at(uses))
                    v.scalar_tensor_tensor(xe[i % RING][:, 0:n_], pqb[slot][:, 0, lo:lo + n_], sd[:, k, bass.ds(rh, 1)],
                                           pqb[slot][:, 1, lo:lo + n_], ALU.add, ALU.max).then_inc(s.x_ready.sem, 1)

                def weights(n, i, k, rel, lo, n_):
                    dve.wait_ge(*s.exp_done.at(n + 1))
                    v.scalar_tensor_tensor(xe[i % RING][:, 0:n_], xe[i % RING][:, 0:n_], 3.0e38,
                                           counts[:, rel, k, lo:lo + n_], ALU.min, ALU.mult).then_inc(s.p_ready.sem, 1)

                def normalise(z_ap, count, two):
                    o = zc[:, 0:count].rearrange("p (a b) -> p a b", b=5) if two else zc[:, 0:count]
                    if c.eps:
                        return v.tensor_scalar(o, z_ap, EPS_Z, None, ALU.add)
                    return v.tensor_scalar(o, z_ap, 1.0e-30, None, ALU.max)

                return exponents, weights, normalise

            def attention(ci, c, ph):
                s = sems[c]
                H, R = c.heads, c.R
                exponents, weights, normalise = layer(ci, c, ph)
                if c is not DD:
                    body = c.unroll * R
                    S_ = body * T
                    with trips(dve, c) as it:
                        def head_rel(i):
                            m = i // T
                            return m, m // R, m % R

                        def make_x(i):
                            m, u, r = head_rel(i)
                            exponents(it * S_ + i, i, i % T, r * H + it * c.unroll + u, m % 2,
                                      it * (8 * body) + 16 * (m // 2 + 1), 0, NP)

                        def save(u):
                            hi = it * c.unroll + u
                            dve.wait_ge(*s.p_used.at(hi * (R * T) + (RING + R * T)))
                            if c is B:
                                z = ps[:, 0:1024].rearrange("p (b c) -> p b c", b=2)[:, :, 0:490] \
                                    .rearrange("p b (t c) -> p b t c", c=98)[:, :, :, 0]
                            else:
                                z = ps[:, 0:5 * 512].rearrange("p (t c) -> p t c", c=256)[:, :, 0]
                            normalise(z, T, c is B).then_inc(s.z_done.sem, 1)
                            dve.wait_ge(*s.z_done.at(hi * 2 + 1))
                            v.reciprocal(rz[:, 0:T], zc[:, 0:T]).then_inc(s.z_done.sem, 1)
                            dve.wait_ge(*s.z_done.at(hi * 2 + 2))
                            for t in range(T):
                                a = sums_at(c, t)
                                v.scalar_tensor_tensor(featv[:, t, bass.ds(hi * c.width, c.width)],
                                                       a[:, 1:1 + c.width], rz[:, t:t + 1],
                                                       brow[:, bass.ds(hi * c.width, c.width)],
                                                       ALU.mult, ALU.add).then_inc(s.saved.sem, 1)

                        make_x(0)
                        for i in range(S_):
                            if i + 1 < S_:
                                make_x(i + 1)
                            m, u, r = head_rel(i)
                            weights(it * S_ + i, i, i % T, c.rels[r], 0, NP)
                            if i % (R * T) == 0 and i:
                                save(u - 1)
                        save(c.unroll - 1)
                else:
                    def exps(j):
                        g, r, k = j // (R * T), j // T % R, j % T
                        exponents(j, j, k, r, (g * R + r) % 2, 16 * ((g * R + r) // 2 + 1),
                                  D_GROUPS[g][0] * P, D_GROUPS[g][1] * P)
                    total = len(D_GROUPS) * R * T
                    exps(0)
                    for g, (t0, nt) in enumerate(D_GROUPS):
                        for r in range(R):
                            for k in range(T):
                                j = (g * R + r) * T + k
                                if j + 1 < total:
                                    exps(j + 1)
                                weights(j, j, k, c.rels[r], t0 * P, nt * P)
                        dve.wait_ge(*s.p_used.at(RING + (g + 1) * R * T))
                        z = ps[:, 0:nt * 1024].rearrange("p (t c) -> p t c", c=1024)[:, :, 0]
                        link(normalise(z, nt, False))
                        link(v.reciprocal(rz[:, 0:nt], zc[:, 0:nt]))
                        for q in range(nt):
                            v.scalar_tensor_tensor(featv[:, t0 + q, 0:384], bank(2 * q, 384, 1), rz[:, q:q + 1],
                                                   brow[:, 0:384], ALU.mult, ALU.add)
                            v.scalar_tensor_tensor(featv[:, t0 + q, 384:768], bank(2 * q + 1, 384), rz[:, q:q + 1],
                                                   brow[:, 384:768], ALU.mult, ALU.add).then_inc(s.saved.sem, 1)

            attention(0, A, 3)
            end_phase(dve, 4)
            attention(1, B, 5)
            end_phase(dve, 6)

            dve.wait_ge(y_in, 16 * 5)
            for t in range(T):
                rn = P if t < T - 1 else LAST
                x = featv[:, t, :]
                halves = lambda ap: ap.rearrange("p (q c) -> p q c", q=2)
                dve.wait_ge(y_mm, t + 1)
                v.tensor_tensor(halves(x), halves(ps[:, t % 3 * 1024:(t % 3 + 1) * 1024])[:, :, 0:384], halves(brow[:, :]),
                                ALU.add).then_inc(y_mm_used, 1)
                dve.wait_ge(y_mm_used, t + 1)
                dve.wait_ge(y_x, 16 * (8 if t < 8 else T))
                link(v.tensor_tensor(featv[0:rn, t, :], featv[0:rn, t, :], spare[t % 8][0:rn, :], ALU.add))
                norm_stats(x, t, y_std)
                dve.wait_ge(y_sqrt, t + 1)
                norm_apply(x, x, t).then_inc(y_done, 1)
            end_phase(dve, 7)

            attention(2, C, 8)
            end_phase(dve, 9)
            attention(3, DD, 10)
            end_phase(dve, 11)

            for t in range(T):
                x = featv[:, t, :]
                dve.wait_ge(f_x[t % 2], 16 * (t // 2 + 1))
                link(v.tensor_tensor(x, x, xe[t % 2][:, 0:D], ALU.add))
                norm_stats(x, t, f_std)
                dve.wait_ge(f_sqrt, t + 1)
                norm_apply(x, x, t).then_inc(f_done, 1)


_INPUTS = ["x", "x_t", "src", "dst", "edge_type", "dst_rows", "norm_g", "norm_b", "al1", "al2", "qk1", "qk2",
           "wt_a", "wt_b", "wt_c", "wt_d", "w_a", "w_b", "w_c", "w_d", "Wu", "bias_a", "bias_b", "bias_c",
           "bias_d", "bias_u"]


def kernel(**inputs):
    import concourse.bacc as bacc
    from concourse.bass_utils import run_bass_kernel_spmd

    a = {k: np.asarray(v) for k, v in inputs.items()}
    edges = lambda v: v.reshape(NCH, EC).T
    lay = {
        "x": a["x"], "x_t": a["x"].T,
        "src": edges(a["src"]), "dst": edges(a["dst"]), "edge_type": edges(a["edge_type_3"]),
        "dst_rows": a["dst"].reshape(NCH, EC),
        "norm_g": a["L0_gnn_norm_g"], "norm_b": a["L0_gnn_norm_b"],
        "al1": np.stack([a["L0_gnn_a_src1"], a["L0_gnn_a_dst1"]]).reshape(2, 8, 96).transpose(2, 1, 0),
        "al2": np.stack([a["L0_gnn_a_src2"], a["L0_gnn_a_dst2"]]).reshape(2, 2, 96).transpose(2, 1, 0),
        "qk1": np.concatenate([a["L1_gnn_k1"], a["L1_gnn_q1"]], 1).reshape(DT, P, 8).transpose(1, 0, 2),
        "qk2": np.concatenate([a["L1_gnn_k2"], a["L1_gnn_q2"]], 1).reshape(DT, P, 2).transpose(1, 0, 2),
        "wt_a": a["L0_gnn_W1"].T, "wt_b": a["L0_gnn_W2"].T,
        "wt_c": a["L1_gnn_W1"].transpose(0, 2, 1), "wt_d": a["L1_gnn_W2"].transpose(0, 2, 1),
        "w_a": a["L0_gnn_W1"], "w_b": a["L0_gnn_W2"],
        "w_c": a["L1_gnn_W1"].reshape(RELS * D, D), "w_d": a["L1_gnn_W2"].reshape(RELS * D, D),
        "Wu": a["L0_gnn_Wu"],
        "bias_a": a["L0_gnn_b1"], "bias_b": a["L0_gnn_b2"], "bias_c": a["L1_gnn_b1"], "bias_d": a["L1_gnn_b2"],
        "bias_u": a["L0_gnn_bu"],
    }
    nc = bacc.Bacc("TRN2", target_bir_lowering=False, num_devices=1)
    arrays, t_in = {}, {}
    for name in _INPUTS:
        v = np.ascontiguousarray(lay[name])
        arrays[f"in_{name}"] = v
        t_in[name] = nc.dram_tensor(f"in_{name}", v.shape, mybir.dt.from_np(v.dtype), kind="ExternalInput").ap()
    out = nc.dram_tensor("out", (N, D), F32, kind="ExternalOutput").ap()
    gnn_program(nc, t_in, out)
    r = run_bass_kernel_spmd(nc, [arrays], core_ids=[0])
    return r.results[0]["out"]
```

```python
from contextlib import ExitStack, contextmanager

import numpy as np

import concourse.bass as bass
from concourse import mybir

F32 = mybir.dt.float32
F16 = mybir.dt.float16
BF16 = mybir.dt.bfloat16
I32 = mybir.dt.int32
U16 = mybir.dt.uint16
ALU = mybir.AluOpType
ACT = mybir.ActivationFunctionType
AX = mybir.AxisListType

P = 128
N = 1250
D = 768
T = (N + P - 1) // P
NP = T * P
LAST = N - (T - 1) * P
DT = D // P
NE = 40000
EC = 125
NCH = NE // EC
W = 16
W_SHIFT = 4
NW = NP // W
WROW = T * 3 * W
WKEY = 512
SRC_SHIFT = 7
TAB_C0 = 96
RELS = 3
TOTAL = RELS
BIG = 1.0e30
EPS_LN = 1e-5
EPS_Z = 1e-16
WCH = 6
OH = 2
ALO = 3
BANKS = 4


class Conv:

    def __init__(self, name, rels, heads, width, v_at, unroll, loops, eps, rows_left):
        self.name, self.rels, self.heads, self.width = name, rels, heads, width
        self.R, self.RH = len(rels), len(rels) * heads
        self.F = heads * width
        self.v_at = v_at
        self.unroll = unroll
        self.loops = loops
        self.piece = min(384, self.F)
        self.pieces = [(r, c) for r in range(self.R) for c in range(0, self.F, self.piece)]
        self.eps = eps
        self.s_rows_at = 0 if name == "a" else T + 1 if len(self.pieces) > 1 else T
        self.pq_rows_at = len(self.pieces) * T - rows_left

    def columns(self, i):
        return self.piece + (2 * self.RH if i == 0 and self.name != "a" else 0)


A = Conv("a", [TOTAL], 4, 192, 0, 4, 1, False, 0)
B = Conv("b", [TOTAL], 2, 96, 8, 2, 1, False, 0)
C = Conv("c", [0, 1, 2], 4, 192, 12, 2, 2, True, 0)
DD = Conv("d", [0, 1, 2], 1, 768, 36, 1, 1, True, 8)
CONVS = [A, B, C, DD]
VCOLS = 42
D_GROUPS = [(0, 4), (4, 4), (8, 2)]
RING = 5
MAXG = NW * NCH
STEP_CREDIT = 30
SAVE_AFTER = 2
Y_FIRST = 3
SHARED = 4


def gnn_program(nc, t_in, out):
    with ExitStack() as ctx:
        def sb(name, shape, dt):
            return ctx.enter_context(nc.sbuf_tensor(name, shape, dt))

        def sem(name):
            return ctx.enter_context(nc.semaphore(name))

        def dram(name, shape, dt):
            return nc.dram_tensor(name, shape, dt, kind="Internal").ap()

        hx_d = dram("hx_d", [RELS * NP, D], F32)
        nomask_d = dram("nomask_d", [4 * NP, NP], BF16)
        srow_d = dram("srow_d", [4 * 12, NP], F32)
        pqrow_d = dram("pqrow_d", [4 * 24, NP], F32)
        x1_d = dram("x1_d", [NP, D], F32)

        counts = sb("counts", [P, 4, T, NP], U16)
        feat = sb("feat", [P, T * D], F32)
        work = sb("work", [P, 16648], F32)
        identf = sb("identf", [P, P], F32)
        identb = sb("identb", [P, P], BF16)
        vtab = sb("vtab", [P, DT, VCOLS], F32)
        sd = sb("sd", [P, T, 24], F32)
        s02 = sb("s02", [P, T, 12], F32)
        mx = sb("mx", [P, T, 12], F32)
        lk = sb("lk", [P, T, 12], F32)
        mm_ = sb("mm_", [P, T, 4], F32)
        pq = sb("pq", [P, T, 24], F32)
        brow = sb("brow", [P, D], F32)
        zc = sb("zc", [P, 16], F32)
        rz = sb("rz", [P, 16], F32)
        stat = sb("stat", [P, T, 2, 6], F32)
        mv = sb("mv", [P, T, 2], F32)
        sdev = sb("sdev", [P, 2, T], F32)
        epsc = sb("epsc", [P, 1], F32)
        winoff = sb("winoff", [P, NW], F32)
        tab = sb("tab", [1, 192], I32)

        ps = ctx.enter_context(nc.psum_tensor("ps", [P, 8 * 512], F32))

        def bank(b, n=512, at=0):
            return ps[:, b * 512 + at:b * 512 + at + n]

        def carve(region, at, n, dt=F32):
            v = region[:, at:at + n]
            return v if dt == F32 else v.bitcast(dt)

        featv = feat[:, :].rearrange("p (t f) -> p t f", t=T)
        xT = carve(work, 0, DT * NP).rearrange("p (j n) -> p j n", j=DT)
        XT_END = DT * NP
        flat_f = [counts[:, i, :, :].rearrange("p t n -> p (t n)").bitcast(F32) for i in range(4)]
        x_tiles = [flat_f[t // 8][:, t % 8 * D:(t % 8 + 1) * D] for t in range(T)]
        grow, nbrow = flat_f[1][:, 2 * D:3 * D], flat_f[1][:, 3 * D:4 * D]
        wt_a, wt_b = flat_f[TOTAL][0:96, 0:8 * D], flat_f[2][0:96, 0:2 * D]
        space = [XT_END]

        def take(n, dt=F32):
            v = carve(work, space[0], n, dt)
            space[0] += n
            return v

        src_i, dst_i, typ_i, win_i, tile_i = (take(NCH, I32) for _ in range(5))
        lof, nlof, keyf = take(NCH), take(NCH), take(NCH)
        dstc, winc = (take(3 * EC, I32).rearrange("p (a e) -> p a e", a=3) for _ in range(2))
        cmin, cmax, cid, cidm, cidp = (take(4)[:, 0:3] for _ in range(5))
        iota_w, tmp_w = take(NW), take(NW)
        act_w = take(6 * NW).rearrange("p (s a w) -> p s a w", s=2, a=3)
        bcol = take(8)
        brow_w = take(3 * NW + 8)
        iota_lo, iota_hi = take(P // 2, F16), take(WROW // 2, F16)
        lo_all = take((OH * WCH + 1) * P // 2, BF16)
        oh_lo = [lo_all[:, i * P:(i + 1) * P] for i in range(OH * WCH + 1)]
        lo_abs = take(ALO * P // 2, F16)
        oh_hi = [take(WROW // 2, BF16) for _ in range(OH * WCH + 1)]
        MH = NP // 2
        nomask_h = [carve(feat, i * T * MH // 2, T * MH // 2, BF16).rearrange("p (k n) -> p k n", k=T) for i in range(2)]
        nm_out = [carve(work, XT_END + i * (NP // 2), NP // 2, BF16) for i in range(3)]
        WTH = DT * (D // 2)
        wt_half = [carve(feat, i * WTH, WTH) for i in range(3)] + \
                  [carve(work, XT_END + 3 * (NP // 2) + i * WTH, WTH) for i in range(3)] * 3
        wt_half = [v.rearrange("p (f d) -> p f d", f=DT) for v in wt_half]
        WT_HALVES = [(c, r, h) for c in (C, DD) for r in range(RELS) for h in range(2)]
        v_rows = [carve(feat, 3 * WTH + i * (D // 2), D // 2) for i in range(2)]
        V_COLS_AT = 96
        space[0] = max(space[0], XT_END + 3 * (NP // 2) + 3 * WTH)
        qk1 = take(DT * 8).rearrange("p (j c) -> p j c", j=DT)
        qk2 = take(DT * 2).rearrange("p (j c) -> p j c", j=DT)
        al1 = take(16).rearrange("p (j c) -> p j c", j=8)
        al2 = take(4).rearrange("p (j c) -> p j c", j=2)
        assert space[0] <= 16648
        wring = [carve(work, XT_END, DT * 408), carve(work, XT_END + DT * 408, DT * 384)]
        o0 = XT_END + DT * (408 + 384)
        nm_in = [carve(work, o0 + i * (NP // 2), NP // 2, BF16) for i in range(3)]
        o1 = o0 + 3 * (NP // 2)
        stage = [carve(work, o1 + i * 384, 384) for i in range(3)]
        junk = [carve(feat, 5 * NP, NP // 2, BF16), carve(work, o1 + 3 * 384, NP // 2, BF16)]
        wu = carve(work, XT_END, DT * D).rearrange("p (j c) -> p j c", j=DT)
        o2T = carve(work, XT_END + DT * D, 2 * NP).rearrange("p (j n) -> p j n", j=2)
        wu_tail = carve(work, XT_END + DT * D + 2 * NP, 2 * D).rearrange("p (j c) -> p j c", j=2)
        assert o1 + 3 * 384 + NP // 2 <= 16648
        spare = [flat_f[TOTAL][:, i * D:(i + 1) * D] for i in range(8)]
        sbc = [v.rearrange("p (h n) -> p h n", h=4) for v in (carve(feat, 0, 4 * NP), flat_f[TOTAL][:, 0:4 * NP])]
        rows = carve(feat, 4 * NP, NP)
        xe = [carve(work, i * NP, NP) for i in range(RING)]
        pqb = [carve(work, (RING + 2 * i) * NP, 2 * NP).rearrange("p (c n) -> p c n", c=2) for i in range(2)]
        hx_all = carve(work, (RING + 4) * NP, RING * 769).rearrange("p (s c) -> p s c", s=RING)
        assert (RING + 4) * NP + RING * 769 <= 16648

        phase = sem("phase")
        phases = [0]
        s_const, s_in, s_chunkin = sem("s_const"), sem("s_in"), sem("s_chunkin")
        s_dve, s_last = sem("s_dve"), sem("s_last")
        x_in = [sem(f"x_in{i}") for i in range(2)]
        ln_std, ln_sqrt, ln_done, ln_turned, ln_copied = (sem(f"ln_{n}") for n in "std sqrt done turned copied".split())
        wt_ab_in = sem("wt_ab_in")
        wt_first = sem("wt_first")
        wt_in = [sem(f"wt_in{i}") for i in range(3)]
        v_done, v_copied, v_turned = sem("v_done"), sem("v_copied"), sem("v_turned")
        bnd_ready, bnd_turned = sem("bnd_ready"), sem("bnd_turned")
        oh_ready, oh_used, win_saved = sem("oh_ready"), sem("oh_used"), sem("win_saved")
        extra_ready, extra_used = sem("extra_ready"), sem("extra_used")
        lo_dist, lo_ready = sem("lo_dist"), sem("lo_ready")
        nm_ready, nm_turned, nm_copied = sem("nm_ready"), sem("nm_turned"), sem("nm_copied")
        nm_out_s = [sem(f"nm_out_s{i}") for i in range(3)]

        v_in, sd_mm, sd_done, srow_t, srow_c, srow_out = (sem(n) for n in "v_in sd_mm sd_done srow_t srow_c srow_out".split())
        pq_ready, pq_t, pq_c, pq_out = (sem(n) for n in "pq_ready pq_t pq_c pq_out".split())
        bias_in, ones = sem("bias_in"), sem("ones")

        class Signal:

            def __init__(self, sem_, before):
                self.sem, self.before = sem_, before

            def at(self, n):
                return self.sem, n + self.before

        class Shared:

            def __init__(self, name):
                self.sem, self.total = sem("layers_" + name), 0

            def layer(self, count):
                self.total += count
                return Signal(self.sem, self.total - count)

        shared = {n: Shared(n) for n in "turned xt_done proj_mm proj_ev max_done x_ready exp_done p_ready p_used "
                  "z_done saved".split()}
        rings = {n: [Shared(f"{n}{i}") for i in range(k)]
                 for n, k in (("w_in", 2), ("nm_in", 3), ("hx_out", 3), ("pq_in", 2), ("s_in", 2), ("hx_in", RING))}

        def ring_share(n, i, size):
            return (n - i + size - 1) // size

        class LayerSems:

            def __init__(self, c):
                turned = 0 if c is A else T
                projected = len(c.pieces) * T
                groups = len(D_GROUPS) if c is DD else c.heads
                steps = groups * c.R * T
                self.turned, self.xt_done = shared["turned"].layer(turned), shared["xt_done"].layer(turned)
                self.proj_mm, self.proj_ev = shared["proj_mm"].layer(projected), shared["proj_ev"].layer(projected)
                self.max_done = shared["max_done"].layer(c.RH * T)
                self.x_ready, self.exp_done = shared["x_ready"].layer(steps), shared["exp_done"].layer(steps)
                self.p_ready, self.p_used = shared["p_ready"].layer(steps), shared["p_used"].layer(steps)
                self.z_done = shared["z_done"].layer(0 if c is DD else 2 * c.heads)
                self.saved = shared["saved"].layer(c.heads * T)
                self.s_in = [q.layer(16 * ring_share(c.R, i, 2)) for i, q in enumerate(rings["s_in"])]
                self.w_in = [q.layer(16 * ring_share(len(c.pieces), i, 2)) for i, q in enumerate(rings["w_in"])]
                self.nm_in = [q.layer(16 * ring_share(c.R * T, i, 3)) for i, q in enumerate(rings["nm_in"])]
                self.hx_out = [q.layer(16 * ring_share(projected, i, 3)) for i, q in enumerate(rings["hx_out"])]
                self.pq_in = [q.layer(16 * ring_share(groups * c.R, i, 2)) for i, q in enumerate(rings["pq_in"])]
                self.hx_in = [q.layer(16 * steps // RING) for q in rings["hx_in"]]

        sems = {c: LayerSems(c) for c in CONVS}
        y_mm_used = sem("y_mm_used")
        y_in, y_x, y_turned, y_copied, y_mm = (sem(f"y_{n}") for n in "in x turned copied mm".split())
        y_xt = [sem(f"y_xt{i}") for i in range(2)]
        y_std, y_sqrt, y_done = sem("y_std"), sem("y_sqrt"), sem("y_done")
        y_out = sem("y_out")
        elu_e, elu_done, elu_min = sem("elu_e"), sem("elu_done"), sem("elu_min")
        f_x = sem("f_x")
        f_std, f_sqrt, f_done, f_out = sem("f_std"), sem("f_sqrt"), sem("f_done"), sem("f_out")

        def end_phase(eng, k):
            eng.drain().then_inc(phase, 1)
            eng.wait_ge(phase, 5 * (k + 1))

        @contextmanager
        def trips(eng, c):
            if c.loops == 1:
                yield 0
            else:
                with eng.Fori(0, c.loops) as it:
                    yield it

        def sums_at(c, t, h):
            if c is B:
                b, at = h % 2 * 2 + t // 5, t % 5 * 98
            else:
                b, at = (2 + 3 * (h % 2) + t // 2 if t < T - SHARED else (t - (T - SHARED)) // 2), t % 2 * 256
            return ps[:, b * 512 + at:b * 512 + at + 1 + c.width]

        def tiles_per_bank(c):
            return 5 if c is B else 2

        block = ctx.enter_context(nc.Block())

        @block.sync
        def _(sp):
            sp.dma_start(dstc[:, 0:2, :], t_in["dst_rows"][0:2 * P, :].rearrange("(a p) e -> p a e", p=P)).then_inc(s_chunkin, 16)
            sp.dma_start(dstc[0:NCH - 2 * P, 2, :], t_in["dst_rows"][2 * P:NCH, :]).then_inc(s_chunkin, 16)
            for a, b in ((src_i, "src"), (dst_i, "dst"), (typ_i, "edge_type")):
                sp.dma_start(a[0:EC, :], t_in[b]).then_inc(s_in, 16)
            sp.dma_start(grow, t_in["norm_g"].partition_broadcast(P)).then_inc(s_in, 16)
            sp.dma_start(nbrow, t_in["norm_b"].partition_broadcast(P)).then_inc(s_in, 16)
            for n, v in (("qk1", qk1), ("qk2", qk2)):
                sp.dma_start(v, t_in[n]).then_inc(s_in, 16)
            for n, v in (("al1", al1), ("al2", al2)):
                sp.dma_start(v[0:96], t_in[n]).then_inc(s_in, 16)
            sp.dma_start(wt_b.rearrange("p (f d) -> p f d", f=2), t_in["wt_b"].rearrange("(f p) d -> p f d", p=96)).then_inc(wt_ab_in, 16)
            for t in range(T):
                rows_n = P if t < T - 1 else LAST
                if t == T - 1:
                    sp.wait_ge(s_last, 1)
                sp.dma_start(x_tiles[t][0:rows_n, :], t_in["x"][t * P:t * P + rows_n, :]).then_inc(x_in[2 * t // T], 16)
            end_phase(sp, 0)
            end_phase(sp, 1)

            for n in range(4 * T):
                sp.wait_ge(nm_copied, n + 1)
                row = (n // T + 1) % 4 * T + n % T
                sp.dma_start(nomask_d[row * P:(row + 1) * P, :], nm_out[n % 3]).then_inc(nm_out_s[n % 3], 16)
            for i in range(3):
                sp.wait_ge(nm_out_s[i], 16 * ring_share(4 * T, i, 3))
            end_phase(sp, 2)

            def layer(ci, c, ph):
                s = sems[c]
                def mask_load(n):
                    r, t = n // T, n % T
                    row = (0 if c.rels[r] == TOTAL else c.rels[r] + 1) * NP + t * P
                    sp.dma_start(nm_in[n % 3], nomask_d[row:row + P, :]).then_inc(s.nm_in[n % 3].sem, 16)

                for n in range(3):
                    mask_load(n)
                sp.wait_ge(srow_c, ci + 1)
                sp.dma_start(srow_d[12 * ci:12 * ci + c.RH, :], rows[0:c.RH, :]).then_inc(srow_out, 16)
                sp.wait_ge(srow_out, 16 * (ci + 1))
                def s_load(r):
                    sp.dma_start(sbc[r % 2][:, 0:c.heads, :].rearrange("p h n -> p (h n)"),
                                 srow_d[12 * ci + r * c.heads:12 * ci + (r + 1) * c.heads, :].rearrange("h n -> (h n)")
                                 .partition_broadcast(P)).then_inc(s.s_in[r % 2].sem, 16)

                for r in range(min(2, c.R)):
                    s_load(r)
                for n in range(3, c.R * T):
                    sp.wait_ge(*s.max_done.at((n - 2) * c.heads))
                    mask_load(n)
                    if n == T + 3 and c.R > 2:
                        s_load(2)
                sp.wait_ge(pq_c, ci + 1)
                sp.dma_start(pqrow_d[24 * ci:24 * ci + 2 * c.RH, :], rows[0:2 * c.RH, :]).then_inc(pq_out, 16)
                sp.wait_ge(pq_out, 16 * (ci + 1))
                sp.dma_start(brow[:, 0:c.F], t_in["bias_" + c.name].partition_broadcast(P)).then_inc(bias_in, 16)
                end_phase(sp, ph)

                def pq_load(slot, rh, cols, used):
                    sp.wait_ge(*s.x_ready.at(used))
                    lo, n_ = cols
                    sp.dma_start(pqb[slot][:, :, lo:lo + n_], pqrow_d[bass.ds(24 * ci + rh * 2, 2), lo:lo + n_]
                                 .partition_broadcast(P)).then_inc(s.pq_in[slot].sem, 16)

                def hx_load(n, i, r, k, col):
                    sp.wait_ge(*s.p_used.at(n + 1))
                    sp.dma_start(hx_all[:, i % RING, 1:1 + c.width],
                                 hx_d[(r * T + k) * P:(r * T + k + 1) * P, bass.ds(col, c.width)]) \
                        .then_inc(s.hx_in[i % RING].sem, 16)

                if c is not DD:
                    body = c.unroll * c.R
                    with trips(sp, c) as it:
                        def pq_next(m):
                            pq_load(m % 2, m % c.R * c.heads + it * c.unroll + m // c.R, (0, NP),
                                    it * (body * T) + (STEP_CREDIT + (m - 1) * T))

                        pq_next(0)
                        for m in range(body):
                            u, r = m // c.R, m % c.R
                            h = it * c.unroll + u
                            for k in range(T):
                                if k == 2 and m + 1 < body:
                                    pq_next(m + 1)
                                i = m * T + k
                                hx_load(it * (body * T) + i, i, r, k, h * c.width)
                else:
                    def out_rows(a, b):
                        for t in range(a, b):
                            rn = P if t < T - 1 else LAST
                            sp.wait_ge(f_done, t + 1)
                            sp.dma_start(out[t * P:t * P + rn, :], featv[0:rn, t, :]).then_inc(f_out, 16)

                    def x1_load(t):
                        sp.dma_start(spare[t % 8], x1_d[t * P:(t + 1) * P, :]).then_inc(f_x, 16)

                    def pq_next(m):
                        t0, nt = D_GROUPS[m // c.R]
                        pq_load(m % 2, m % c.R, (t0 * P, nt * P), STEP_CREDIT + (m - 1) * T)

                    pq_next(0)
                    for g, (t0, nt) in enumerate(D_GROUPS):
                        for r in range(c.R):
                            if g == 0 and r == 1:
                                for t in range(8):
                                    x1_load(t)
                            if g and r == 2:
                                out_rows(*before)
                            if g == 1 and r == 2:
                                for t in range(8, T):
                                    x1_load(t)
                            for k in range(T):
                                if k == 2 and g * 3 + r + 1 < len(D_GROUPS) * c.R:
                                    pq_next(g * 3 + r + 1)
                                i = (g * 3 + r) * T + k
                                hx_load(i, i, r, k, 0)
                        before = (t0, t0 + nt)
                    out_rows(*before)
                    sp.wait_ge(f_out, 16 * T)

            layer(0, A, 3)
            end_phase(sp, 4)
            layer(1, B, 5)
            end_phase(sp, 6)

            sp.dma_start(brow[:, :], t_in["bias_u"].partition_broadcast(P)).then_inc(y_in, 16)
            sp.dma_start(wu, t_in["Wu"][0:D, :].rearrange("(j p) c -> p j c", p=P)).then_inc(y_in, 16)
            sp.dma_start(wu_tail[:, 0, :], t_in["Wu"][D:D + P, :]).then_inc(y_in, 16)
            sp.dma_start(wu_tail[0:64, 1, :], t_in["Wu"][D + P:D + 192, :]).then_inc(y_in, 16)
            x_t = t_in["x_t"].rearrange("(j p) n -> p j n", p=P)
            sp.dma_start(xT[:, :, 0:Y_FIRST * P], x_t[:, :, 0:Y_FIRST * P]).then_inc(y_xt[0], 16)
            sp.dma_start(xT[:, :, Y_FIRST * P:N], x_t[:, :, Y_FIRST * P:N]).then_inc(y_xt[1], 16)

            def x_load(t):
                rn = P if t < T - 1 else LAST
                sp.dma_start(spare[t % 8][0:rn, :], t_in["x"][t * P:t * P + rn, :]).then_inc(y_x, 16)

            for t in range(8):
                x_load(t)
            for t in range(T):
                sp.wait_ge(y_done, t + 1)
                if t < T - 8:
                    x_load(t + 8)
                sp.dma_start(x1_d[t * P:(t + 1) * P, :], featv[:, t, :]).then_inc(y_out, 16)
            sp.wait_ge(y_out, 16 * T)
            end_phase(sp, 7)

            layer(2, C, 8)
            end_phase(sp, 9)
            layer(3, DD, 10)

        @block.gpsimd
        def _(pool):
            def then(ins):
                pool_n[0] += 1
                ins.then_inc(s_const, 1)
                return pool_n[0]
            pool_n = [0]
            then(nc.gpsimd.memset(identf[:, :], 0.0))
            then(nc.gpsimd.memset(identb[:, :], 0.0))
            pool.wait_ge(s_const, 2)
            then(nc.gpsimd.affine_select(out=identf[:, :], in_=identf[:, :], compare_op=ALU.not_equal, fill=1.0,
                                         base=0, pattern=[[-1, P]], channel_multiplier=1))
            then(nc.gpsimd.affine_select(out=identb[:, :], in_=identb[:, :], compare_op=ALU.not_equal, fill=1.0,
                                         base=0, pattern=[[-1, P]], channel_multiplier=1))
            then(nc.gpsimd.memset(epsc[:, :], EPS_LN))
            imp = dict(allow_small_or_imprecise_dtypes=True)
            then(nc.gpsimd.iota(iota_lo, [[1, P]], base=0, channel_multiplier=0, **imp))
            then(nc.gpsimd.iota(iota_hi, [[1, WROW]], base=0, channel_multiplier=0, **imp))
            then(nc.gpsimd.iota(winoff[:, :], [[WKEY, NW]], base=0, channel_multiplier=0, **imp))
            then(nc.gpsimd.iota(iota_w, [[1, NW]], base=0, channel_multiplier=0, **imp))
            then(nc.gpsimd.iota(cid, [[P, 3]], base=0, channel_multiplier=1, **imp))
            assert pool_n[0] == 10
            end_phase(pool, 0)
            end_phase(pool, 1)

            def wt_load(i):
                c, r, h = WT_HALVES[i]
                pool.dma_start(wt_half[i], t_in["wt_" + c.name][r].rearrange("(f p) d -> p f d", p=P)
                               [:, :, h * (D // 2):(h + 1) * (D // 2)]).then_inc(wt_in[i % 3], 16)

            for i in range(3, 12):
                if i >= 6:
                    pool.wait_ge(v_done, 1 + i - 2)
                wt_load(i)
            for k in range(2, 11):
                end_phase(pool, k)

        @block.tensor
        def _(pe):
            mm = nc.tensor.matmul
            pe.wait_ge(s_const, 10)

            pe.wait_ge(bnd_ready, 1)
            for s_ in range(2):
                for a in range(3):
                    last = nc.tensor.transpose(ps[0:NW, (4 + s_) * 512 + a * P:(4 + s_) * 512 + (a + 1) * P],
                                               act_w[:, s_, a, :], identf[:, :])
            last.then_inc(bnd_turned, 1)
            pe.wait_ge(bnd_ready, 2)
            for i in range(2):
                last = nc.tensor.transpose(ps[0:1, 7 * 512 + i * P:7 * 512 + i * P + NW],
                                           bcol[0:NW, i:i + 1], identf[0:NW, 0:NW])
            last.then_inc(bnd_turned, 1)

            pe.wait_ge(s_in, 16 * 9)
            pe.wait_ge(wt_ab_in, 32)
            for c, wt, al, per, at in ((A, wt_a, al1, 2, 0), (B, wt_b, al2, 1, 48)):
                for j in range(DT):
                    for h in range(c.heads):
                        for q in range(per):
                            f = h * per + q
                            last = mm(bank(6, 2, at + (j * c.heads + h) * 2), wt[:, f * D + j * P:f * D + (j + 1) * P],
                                      al[0:96, f, :], start=(q == 0), stop=(q == per - 1))
            last.then_inc(v_done, 1)
            for t in range(T):
                pe.wait_ge(ln_done, t + 1)
                if t >= 2:
                    pe.wait_ge(ln_copied, t - 1)
                for j in range(DT):
                    last = nc.tensor.transpose(ps[:, t % 2 * 1024 + j * P:t % 2 * 1024 + (j + 1) * P],
                                               x_tiles[t][:, j * P:(j + 1) * P], identf[:, :])
                last.then_inc(ln_turned, 1)
            end_phase(pe, 0)

            pe.sem_inc(oh_used, OH)
            pe.sem_inc(extra_used, 1)

            def edge_product(b, slot, start):
                return mm(bank(b, WROW), oh_lo[slot][0:EC, :], oh_hi[slot][0:EC, :],
                          start=start, stop=False, skip_group_check=True)

            def windows(extra):
                with pe.Fori(0, NW // BANKS) as i:
                    for u in range(BANKS):
                        w = i * BANKS + u
                        pe.wait_ge(win_saved, w + 1)
                        pe.wait_ge(lo_ready, w + 1)
                        pe.wait_ge(oh_ready, w + 1)
                        for q in range(WCH):
                            last = edge_product(u, u % OH * WCH + q, q == 0)
                        last.then_inc(oh_used, 1)
                        if extra:
                            e0 = pe.value_load(tab[0:1, bass.ds(w, 1)], min_val=0, max_val=MAXG)
                            e1 = pe.value_load(tab[0:1, bass.ds(w + 1, 1)], min_val=0, max_val=MAXG)
                            with pe.If(e0 < e1):
                                with pe.Fori(e0, e1) as e:
                                    pe.wait_ge(extra_ready, e + 1)
                                    edge_product(u, OH * WCH, False).then_inc(extra_used, 1)

            extras = pe.value_load(tab[0:1, NW:NW + 1], min_val=0, max_val=MAXG)
            with pe.If(extras < 1):
                windows(False)
            with pe.Else():
                windows(True)
            end_phase(pe, 1)

            def score_rows(i):
                c, r, h = WT_HALVES[i]
                if i < 3:
                    pe.wait_ge(wt_first, 48)
                else:
                    pe.wait_ge(wt_in[i % 3], 16 * (i // 3))
                qk = qk1 if c is C else qk2
                for f in range(DT):
                    last = mm(ps[0:2 * c.heads, 6 * 512:6 * 512 + D // 2], qk[:, f, :], wt_half[i][:, f, :],
                              start=(f == 0), stop=(f == DT - 1))
                last.then_inc(v_done, 1)

            def score_columns(i):
                n2 = 2 * WT_HALVES[i][0].heads
                pe.wait_ge(v_copied, i + 1)
                for j in range(DT // 2):
                    last = nc.tensor.transpose(bank(7, n2, V_COLS_AT + i * 24 + j * n2),
                                               v_rows[i % 2][0:n2, j * P:(j + 1) * P], identf[0:n2, 0:n2])
                last.then_inc(v_turned, 1)

            for i in range(3):
                if i:
                    score_columns(i - 1)
                score_rows(i)
            for t in range(T):
                for j in range(DT):
                    last = mm(bank(7, 2 * A.RH, t * 2 * A.RH), xT[:, j, t * P:(t + 1) * P],
                              vtab[:, j, A.v_at:A.v_at + 2 * A.RH], start=(j == 0), stop=(j == DT - 1))
            last.then_inc(sd_mm, 1)
            for q in range(8):
                pe.wait_ge(nm_ready, q + 1)
                for t in range(T // 2):
                    n = q * (T // 2) + t
                    if n >= 3:
                        pe.wait_ge(nm_copied, n - 2)
                    o = ps[:, (n % 3) * 1024:(n % 3) * 1024 + NP // 2].bitcast(BF16)
                    for k in range(T):
                        last = nc.tensor.transpose(o[:, k * P:(k + 1) * P], nomask_h[q % 2][:, k, t * P:(t + 1) * P],
                                                   identb[:, :])
                    last.then_inc(nm_turned, 1)
                score_columns(2 + q)
                score_rows(3 + q)
            score_columns(10)
            score_rows(11)
            score_columns(11)
            end_phase(pe, 2)

            def layer(ci, c, ph, turn):
                s = sems[c]
                if turn:
                    for t in range(T):
                        if t >= 2:
                            pe.wait_ge(*s.xt_done.at(t - 1))
                        if c is DD:
                            pe.wait_ge(elu_done, t + 1)
                        for j in range(DT):
                            last = nc.tensor.transpose(ps[:, (t % 2) * 1024 + j * P:(t % 2) * 1024 + (j + 1) * P],
                                                       featv[:, t, j * P:(j + 1) * P], identf[:, :])
                        last.then_inc(s.turned.sem, 1)
                    pe.wait_ge(*s.xt_done.at(T))
                def turn_rows(ready, columns, number, turned_rows):
                    pe.wait_ge(ready, ci + 1)
                    for t in range(T):
                        last = nc.tensor.transpose(ps[0:number, 5 * 512 + t * P:5 * 512 + (t + 1) * P],
                                                   columns[:, t, 0:number], identf[:, :])
                    last.then_inc(turned_rows, 1)

                n = 0
                for i, (r, cc) in enumerate(c.pieces):
                    pe.wait_ge(*s.w_in[i % 2].at(16 * (i // 2 + 1)))
                    if i == 0 and c is not A:
                        pe.wait_ge(v_in, ci)
                    cols = c.columns(i)
                    wv = wring[i % 2][:, 0:DT * cols].rearrange("p (j c) -> p j c", j=DT)
                    for t in range(T):
                        if n == c.s_rows_at:
                            turn_rows(sd_done, sd, c.RH, srow_t)
                        if n == c.pq_rows_at:
                            turn_rows(pq_ready, pq, 2 * c.RH, pq_t)
                        if n >= 4:
                            pe.wait_ge(*s.proj_ev.at(n - 3))
                        for j in range(DT):
                            last = mm(bank(n % 4, cols), xT[:, j, t * P:(t + 1) * P], wv[:, j, :],
                                      start=(j == 0), stop=(j == DT - 1))
                        last.then_inc(s.proj_mm.sem, 1)
                        n += 1
                if n == c.s_rows_at:
                    turn_rows(sd_done, sd, c.RH, srow_t)
                if n == c.pq_rows_at:
                    turn_rows(pq_ready, pq, 2 * c.RH, pq_t)
                end_phase(pe, ph)
                if c is A:
                    pe.sem_inc(s.p_used.sem, RING)
                pe.wait_ge(ones, ci + 1)
                if c is not DD:
                    body = c.unroll * c.R
                    tb = tiles_per_bank(c)
                    with trips(pe, c) as it:
                        for i in range(body * T):
                            m, k = i // T, i % T
                            u, r = m // c.R, m % c.R
                            n = it * (body * T) + i
                            pe.wait_ge(*s.p_ready.at(n + 1))
                            pe.wait_ge(*s.hx_in[i % RING].at(it * (16 * body * T // RING) + 16 * (i // RING + 1)))
                            for t in range(T):
                                if r == 0 and k == 0 and t % tb == 0:
                                    ahead = t - (T - SHARED) + tb if c is not B and t >= T - SHARED else 0
                                    pe.wait_ge(*s.saved.at((it * c.unroll + u) * T + (T + ahead)))
                                last = mm(sums_at(c, t, u), xe[i % RING][:, t * P:(t + 1) * P],
                                          hx_all[:, i % RING, 0:1 + c.width],
                                          start=(r == 0 and k == 0 and t % tb == 0), stop=(r == c.R - 1 and k == T - 1),
                                          skip_group_check=True)
                            last.then_inc(s.p_used.sem, 1)
                else:
                    for g, (t0, nt) in enumerate(D_GROUPS):
                        for r in range(c.R):
                            for k in range(T):
                                i = (g * 3 + r) * T + k
                                pe.wait_ge(*s.p_ready.at(i + 1))
                                pe.wait_ge(*s.hx_in[i % RING].at(16 * (i // RING + 1)))
                                for q in range(nt):
                                    if r == 0 and k == 0 and t0 + q >= 4:
                                        pe.wait_ge(*s.saved.at(2 * T + t0 + q - 4 + 1))
                                    for v, (a, b) in enumerate(((0, 385), (385, 769))):
                                        last = mm(bank(2 * ((t0 + q) % 4) + v, b - a), xe[i % RING][:, q * P:(q + 1) * P],
                                                  hx_all[:, i % RING, a:b],
                                                  start=(r == 0 and k == 0), stop=(r == c.R - 1 and k == T - 1))
                                last.then_inc(s.p_used.sem, 1)

            layer(0, A, 3, False)
            end_phase(pe, 4)
            layer(1, B, 5, True)
            end_phase(pe, 6)

            for t in range(T):
                if t >= 2:
                    pe.wait_ge(y_copied, t - 1)
                for j, n_ in ((0, P), (1, 64)):
                    last = nc.tensor.transpose(ps[0:n_, (6 + t % 2) * 512 + j * P:(6 + t % 2) * 512 + (j + 1) * P],
                                               featv[:, t, j * P:j * P + n_], identf[:, :])
                last.then_inc(y_turned, 1)
            pe.wait_ge(y_copied, T)
            pe.wait_ge(y_in, 16 * 4)
            pe.wait_ge(y_xt[0], 16)
            for t in range(T):
                if t == Y_FIRST:
                    pe.wait_ge(y_xt[1], 16)
                if t >= 3:
                    pe.wait_ge(y_mm_used, t - 2)
                for q in range(2):
                    o = bank(2 * (t % 3) + q, 384)
                    cols = slice(q * 384, (q + 1) * 384)
                    for j in range(DT):
                        mm(o, xT[:, j, t * P:(t + 1) * P], wu[:, j, cols], start=(j == 0), stop=False)
                    mm(o, o2T[:, 0, t * P:(t + 1) * P], wu_tail[:, 0, cols], start=False, stop=False)
                    last = mm(o, o2T[0:64, 1, t * P:(t + 1) * P], wu_tail[0:64, 1, cols], start=False, stop=True)
                last.then_inc(y_mm, 1)
            end_phase(pe, 7)

            layer(2, C, 8, True)
            end_phase(pe, 9)
            layer(3, DD, 10, True)

        @block.scalar
        def _(act):
            act.wait_ge(s_chunkin, 32)
            act.dma_start(wt_a.rearrange("p (f d) -> p f d", f=8), t_in["wt_a"].rearrange("(f p) d -> p f d", p=96)).then_inc(wt_ab_in, 16)
            act.wait_ge(x_in[1], 16 * T // 2)
            for i in range(3):
                c, r, h = WT_HALVES[i]
                act.dma_start(wt_half[i], t_in["wt_" + c.name][r].rearrange("(f p) d -> p f d", p=P)
                              [:, :, h * (D // 2):(h + 1) * (D // 2)]).then_inc(wt_first, 16)
            act.wait_ge(s_const, 10)
            act.wait_ge(ln_std, 1)
            nc.scalar.activation(sdev[:, 0, :], mv[:, :, 1], ACT.Sqrt, bias=epsc[:, 0:1]).then_inc(ln_sqrt, 1)
            for t in range(T):
                act.wait_ge(ln_turned, t + 1)
                nc.scalar.activation(xT[:, :, t * P:(t + 1) * P],
                                     ps[:, t % 2 * 1024:t % 2 * 1024 + D].rearrange("p (j n) -> p j n", j=DT),
                                     ACT.Copy).then_inc(ln_copied, 1)
            end_phase(act, 0)

            act.sem_inc(win_saved, BANKS)
            def one_hot_lo(u, w, free, made):
                c0 = act.value_load(tab[0:1, bass.ds(w + TAB_C0, 1)], min_val=0, max_val=NCH - WCH)
                act.wait_ge(oh_used, free)
                for q in range(ALO):
                    last = nc.scalar.activation(lo_abs[0:EC, q * P:(q + 1) * P], iota_lo[0:EC, :], ACT.Abs,
                                                bias=nlof[0:EC, bass.ds(c0 + q, 1)])
                last.then_inc(lo_dist, 1)
                act.wait_ge(lo_dist, made)
                at = u % OH * WCH * P
                nc.scalar.activation(lo_all[0:EC, at:at + ALO * P], lo_abs[0:EC, :], ACT.Relu, bias=1.0,
                                     scale=-1.0).then_inc(lo_ready, 1)

            def windows(extra):
                one_hot_lo(0, 0, 1, 1)
                with act.Fori(0, NW // BANKS) as i:
                    for u in range(BANKS):
                        w = i * BANKS + u
                        act.wait_ge(lo_ready, w + 1)
                        one_hot_lo(u + 1, w + 1, w + 2, w + 2)
                        act.wait_ge(oh_used, w + (OH + 1))
                        if extra:
                            e1 = act.value_load(tab[0:1, bass.ds(w + 1, 1)], min_val=0, max_val=MAXG)
                            act.wait_ge(extra_used, e1 + 1)
                        sums = bank(u, WROW).rearrange("p (k r x) -> p r k x", k=T, r=3)
                        for r in range(3):
                            last = nc.scalar.activation(counts[:, r, :, bass.ds(w * W, W)], sums[:, r], ACT.Copy)
                        last.then_inc(win_saved, 1)

            extras = act.value_load(tab[0:1, NW:NW + 1], min_val=0, max_val=MAXG)
            with act.If(extras < 1):
                windows(False)
            with act.Else():
                windows(True)
            end_phase(act, 1)

            act.wait_ge(sd_mm, 1)
            sums = bank(7, T * 2 * A.RH).rearrange("p (t c) -> p t c", t=T)
            nc.scalar.activation(s02[:, :, 0:A.RH], sums[:, :, 0:A.RH], ACT.Copy, scale=0.2)
            nc.scalar.activation(sd[:, :, 0:2 * A.RH], sums, ACT.Copy).then_inc(sd_done, 1)
            for n in range(4 * T):
                act.wait_ge(nm_turned, n + 1)
                if n >= 3:
                    act.wait_ge(nm_out_s[n % 3], 16 * (n // 3))
                o = ps[:, (n % 3) * 1024:(n % 3) * 1024 + NP // 2].bitcast(BF16)
                nc.scalar.activation(nm_out[n % 3], o, ACT.Copy).then_inc(nm_copied, 1)
            end_phase(act, 2)

            def layer(ci, c, ph, turn, shift):
                s = sems[c]
                def w_load(i):
                    r, cc = c.pieces[i]
                    src = t_in["w_" + c.name]
                    act.dma_start(wring[i % 2][:, 0:DT * c.columns(i)].rearrange("p (j c) -> p j c", j=DT)[:, :, 0:c.piece],
                                  src[r * D:(r + 1) * D, cc:cc + c.piece].rearrange("(j p) c -> p j c", p=P)) \
                        .then_inc(s.w_in[i % 2].sem, 16)

                w_load(0)
                if len(c.pieces) > 1:
                    w_load(1)
                def elu_exp(t):
                    act.wait_ge(elu_min, t + 1)
                    nc.scalar.activation(spare[t % 8], spare[t % 8], ACT.Exp).then_inc(elu_e, 1)

                if c is DD:
                    elu_exp(0)
                    elu_exp(1)
                if turn:
                    for t in range(T):
                        if c is DD and t + 2 < T:
                            elu_exp(t + 2)
                        act.wait_ge(*s.turned.at(t + 1))
                        nc.scalar.activation(xT[:, :, t * P:(t + 1) * P],
                                             ps[:, (t % 2) * 1024:(t % 2) * 1024 + D].rearrange("p (j n) -> p j n", j=DT),
                                             ACT.Copy, bias=shift).then_inc(s.xt_done.sem, 1)
                def copy_rows(turned_rows, number, copied):
                    act.wait_ge(turned_rows, ci + 1)
                    nc.scalar.activation(rows[0:number, :], ps[0:number, 5 * 512:5 * 512 + NP], ACT.Copy).then_inc(copied, 1)

                n = 0
                for i, (r, cc) in enumerate(c.pieces):
                    for t in range(T):
                        if n == c.s_rows_at:
                            copy_rows(srow_t, c.RH, srow_c)
                        if n == c.pq_rows_at:
                            copy_rows(pq_t, 2 * c.RH, pq_c)
                        act.wait_ge(*s.proj_mm.at(n + 1))
                        if n >= 3:
                            act.wait_ge(*s.hx_out[n % 3].at(16 * (n // 3)))
                        if i == 0 and c is not A:
                            sums = bank(n % 4, 2 * c.RH, c.piece)
                            nc.scalar.activation(s02[:, t, 0:c.RH], sums[:, 0:c.RH], ACT.Copy, scale=0.2)
                            last = nc.scalar.activation(sd[:, t, 0:2 * c.RH], sums, ACT.Copy)
                            if t == T - 1:
                                last.then_inc(sd_done, 1)
                        nc.scalar.activation(stage[n % 3][:, 0:c.piece], bank(n % 4, c.piece), ACT.Copy).then_inc(s.proj_ev.sem, 1)
                        act.wait_ge(*s.proj_ev.at(n + 1))
                        act.dma_start(hx_d[(r * T + t) * P:(r * T + t + 1) * P, cc:cc + c.piece],
                                      stage[n % 3][:, 0:c.piece]).then_inc(s.hx_out[n % 3].sem, 16)
                        n += 1
                    if i + 2 < len(c.pieces):
                        w_load(i + 2)
                if n == c.s_rows_at:
                    copy_rows(srow_t, c.RH, srow_c)
                if n == c.pq_rows_at:
                    copy_rows(pq_t, 2 * c.RH, pq_c)
                for q in range(3):
                    act.wait_ge(*s.hx_out[q].at(16 * ((n - q + 2) // 3)))
                end_phase(act, ph)

                def exp(n, i, k, rh, n_):
                    act.wait_ge(*s.x_ready.at(n + STEP_CREDIT + 1))
                    nc.scalar.activation(xe[i % RING][:, 0:n_], xe[i % RING][:, 0:n_], ACT.Exp,
                                         bias=s02[:, k, bass.ds(rh, 1)], scale=0.8).then_inc(s.exp_done.sem, 1)

                if c is not DD:
                    body = c.unroll * c.R
                    with trips(act, c) as it:
                        for i in range(body * T):
                            m, k = i // T, i % T
                            u, r = m // c.R, m % c.R
                            exp(it * (body * T) + i, i, k, r * c.heads + it * c.unroll + u, NP)
                else:
                    def f_norm(t):
                        act.wait_ge(f_std, t + 1)
                        nc.scalar.activation(sdev[:, 0, t:t + 1], mv[:, t, 1:2], ACT.Sqrt, bias=epsc[:, 0:1]).then_inc(f_sqrt, 1)

                    for g, (t0, nt) in enumerate(D_GROUPS):
                        for r in range(c.R):
                            for k in range(T):
                                i = (g * 3 + r) * T + k
                                exp(i, i, k, r, nt * P)
                                at = k - SAVE_AFTER - 2
                                if g and r == 0 and 0 <= at < before[1]:
                                    f_norm(before[0] + at)
                        before = (t0, nt)
                    for t in range(t0, T):
                        f_norm(t)

            layer(0, A, 3, False, 0.0)
            end_phase(act, 4)
            layer(1, B, 5, True, 0.0)
            end_phase(act, 6)

            for t in range(T):
                act.wait_ge(y_turned, t + 1)
                nc.scalar.activation(o2T[:, 0, t * P:(t + 1) * P], ps[:, (6 + t % 2) * 512:(6 + t % 2) * 512 + P], ACT.Copy)
                nc.scalar.activation(o2T[0:64, 1, t * P:(t + 1) * P],
                                     ps[0:64, (6 + t % 2) * 512 + P:(6 + t % 2) * 512 + 2 * P], ACT.Copy).then_inc(y_copied, 1)
            for t in range(T):
                act.wait_ge(y_std, t + 1)
                nc.scalar.activation(sdev[:, 0, t:t + 1], mv[:, t, 1:2], ACT.Sqrt, bias=epsc[:, 0:1]).then_inc(y_sqrt, 1)
            end_phase(act, 7)

            layer(2, C, 8, True, 0.0)
            end_phase(act, 9)
            layer(3, DD, 10, True, -1.0)

        @block.vector
        def _(dve):
            v = nc.vector
            n_link = [0]

            def link(ins):
                n_link[0] += 1
                ins.then_inc(s_dve, 1)
                dve.wait_ge(s_dve, n_link[0])

            def norm_stats(x, t, std):
                for q in range(2):
                    st = v.bn_stats(stat[:, t, q, :], x[:, q * 384:(q + 1) * 384])
                link(st)
                ins = v.bn_aggr(mv[:, t, :], stat[:, t, :, :].rearrange("p a b -> p (a b)"))
                if std is not None:
                    ins.then_inc(std, 1)
                return ins

            def norm_apply(o, x, t):
                link(v.reciprocal(sdev[:, 1, t:t + 1], sdev[:, 0, t:t + 1]))
                return v.tensor_scalar(o, x, mv[:, t, 0:1], sdev[:, 1, t:t + 1], ALU.subtract, ALU.mult)

            v.memset(x_tiles[T - 1], 0.0).then_inc(s_last, 1)
            v.memset(cmin, 1.0e4)
            link(v.memset(cmax, -1.0))
            dve.wait_ge(s_const, 10)
            dve.wait_ge(s_chunkin, 32)
            tail = NCH - 2 * P
            v.tensor_scalar(winc[:, 0:2, :], dstc[:, 0:2, :], W_SHIFT, None, ALU.logical_shift_right)
            link(v.tensor_scalar(winc[0:tail, 2, :], dstc[0:tail, 2, :], W_SHIFT, None, ALU.logical_shift_right))
            v.tensor_reduce(cmin[:, 0:2], winc[:, 0:2, :], AX.X, ALU.min)
            v.tensor_reduce(cmin[0:tail, 2:3], winc[0:tail, 2, :], AX.X, ALU.min)
            v.tensor_reduce(cmax[:, 0:2], winc[:, 0:2, :], AX.X, ALU.max)
            v.tensor_reduce(cmax[0:tail, 2:3], winc[0:tail, 2, :], AX.X, ALU.max)
            v.tensor_scalar(cidm, cid, -1000.0, None, ALU.add)
            link(v.tensor_scalar(cidp, cid, 1.0, None, ALU.add))
            for a in range(3):
                link(v.tensor_scalar(tmp_w, iota_w, cmin[:, a:a + 1], None, ALU.is_ge))
                link(v.scalar_tensor_tensor(tmp_w, iota_w, cmax[:, a:a + 1], tmp_w, ALU.is_le, ALU.mult))
                v.tensor_scalar(act_w[:, 0, a, :], tmp_w, cidm[:, a:a + 1], 1000.0, ALU.mult, ALU.add)
                link(v.tensor_scalar(act_w[:, 1, a, :], tmp_w, cidp[:, a:a + 1], None, ALU.mult))
            v.nop().then_inc(bnd_ready, 1)
            dve.wait_ge(bnd_turned, 1)
            v.tensor_reduce(bcol[0:NW, 2:3], ps[0:NW, 4 * 512:4 * 512 + 3 * P], AX.X, ALU.min)
            link(v.tensor_reduce(bcol[0:NW, 3:4], ps[0:NW, 5 * 512:5 * 512 + 3 * P], AX.X, ALU.max))
            link(v.tensor_scalar(bcol[0:NW, 0:1], bcol[0:NW, 2:3], float(NCH - WCH), None, ALU.min))
            link(v.tensor_scalar(bcol[0:NW, 4:5], bcol[0:NW, 0:1], float(WCH), None, ALU.add))
            link(v.tensor_tensor(bcol[0:NW, 5:6], bcol[0:NW, 4:5], bcol[0:NW, 3:4], ALU.max))
            link(v.tensor_tensor(bcol[0:NW, 1:2], bcol[0:NW, 5:6], bcol[0:NW, 4:5], ALU.subtract))
            v.nop().then_inc(bnd_ready, 1)
            dve.wait_ge(bnd_turned, 2)
            lo, num, cum = brow_w[0:1, 0:NW], brow_w[0:1, NW:2 * NW], brow_w[0:1, 2 * NW:3 * NW + 1]
            v.memset(cum, 0.0)
            v.memset(tab[:, :], 0)
            v.tensor_copy(lo, ps[0:1, 7 * 512:7 * 512 + NW])
            link(v.tensor_copy(num, ps[0:1, 7 * 512 + P:7 * 512 + P + NW]))
            link(v.tensor_tensor_scan(cum[:, 1:NW + 1], num, num, 0.0, ALU.add, ALU.max))
            v.tensor_copy(tab[:, 0:NW + 1], cum)
            v.tensor_copy(tab[:, TAB_C0:TAB_C0 + NW], lo)
            dve.wait_ge(s_in, 16 * 9)
            v.tensor_scalar(win_i[0:EC, :], dst_i[0:EC, :], W_SHIFT, None, ALU.logical_shift_right)
            link(v.tensor_scalar(tile_i[0:EC, :], src_i[0:EC, :], SRC_SHIFT, None, ALU.logical_shift_right))
            link(v.scalar_tensor_tensor(keyf[0:EC, :], win_i[0:EC, :], float(WKEY - W), dst_i[0:EC, :], ALU.mult, ALU.add))
            link(v.scalar_tensor_tensor(keyf[0:EC, :], typ_i[0:EC, :], float(W), keyf[0:EC, :], ALU.mult, ALU.add))
            link(v.scalar_tensor_tensor(keyf[0:EC, :], tile_i[0:EC, :], float(3 * W), keyf[0:EC, :], ALU.mult, ALU.add))
            v.scalar_tensor_tensor(lof[0:EC, :], tile_i[0:EC, :], -float(P), src_i[0:EC, :], ALU.mult, ALU.add)
            v.scalar_tensor_tensor(nlof[0:EC, :], tile_i[0:EC, :], float(P), src_i[0:EC, :], ALU.mult, ALU.subtract)

            dve.wait_ge(s_last, 1)
            for t in range(T):
                dve.wait_ge(x_in[2 * t // T], 16 * T // 2)
                last = norm_stats(x_tiles[t], t, ln_std if t == T - 1 else None)
            dve.wait_ge(ln_sqrt, 1)
            link(v.reciprocal(sdev[:, 1, :], sdev[:, 0, :]))
            for t in range(T):
                x = x_tiles[t]
                link(v.scalar_tensor_tensor(x, x, mv[:, t, 0:1], grow, ALU.subtract, ALU.mult))
                v.scalar_tensor_tensor(x, x, sdev[:, 1, t:t + 1], nbrow, ALU.mult, ALU.add).then_inc(ln_done, 1)
            dve.wait_ge(v_done, 1)
            for c, at in ((A, 0), (B, 48)):
                for q in range(2):
                    v.tensor_copy(vtab[:, :, c.v_at + q * c.heads:c.v_at + (q + 1) * c.heads],
                                  bank(6, DT * 2 * c.heads, at).rearrange("p (j h q) -> p j h q", j=DT, q=2)[:, :, :, q])
            end_phase(dve, 0)

            def one_hot_lo(slot, ch):
                return v.tensor_scalar(oh_lo[slot][0:EC, :], iota_lo[0:EC, :], lof[0:EC, bass.ds(ch, 1)],
                                         None, ALU.is_equal)

            def one_hot_hi(slot, w, ch):
                return v.tensor_scalar(oh_hi[slot][0:EC, :], iota_hi[0:EC, :], winoff[0:EC, bass.ds(w, 1)],
                                       keyf[0:EC, bass.ds(ch, 1)], ALU.add, ALU.is_equal)

            def windows(extra):
                with dve.Fori(0, NW // BANKS) as i:
                    for u in range(BANKS):
                        w = i * BANKS + u
                        c0 = dve.value_load(tab[0:1, bass.ds(w + TAB_C0, 1)], min_val=0, max_val=NCH - WCH)
                        dve.wait_ge(oh_used, w + 1)
                        for q in range(ALO, WCH):
                            one_hot_lo(u % OH * WCH + q, c0 + q)
                        for q in range(WCH):
                            last = one_hot_hi(u % OH * WCH + q, w, c0 + q)
                        last.then_inc(oh_ready, 1)
                        if extra:
                            e0 = dve.value_load(tab[0:1, bass.ds(w, 1)], min_val=0, max_val=MAXG)
                            e1 = dve.value_load(tab[0:1, bass.ds(w + 1, 1)], min_val=0, max_val=MAXG)
                            with dve.If(e0 < e1):
                                with dve.Fori(e0, e1) as e:
                                    ch = nc.s_assert_within(
                                        e - e0 + c0 + WCH, 0, NCH - 1, skip_runtime_bounds_check_because=
                                        "a window's chunks end with the last chunk at most")
                                    dve.wait_ge(extra_used, e + 1)
                                    one_hot_lo(OH * WCH, ch)
                                    one_hot_hi(OH * WCH, w, ch).then_inc(extra_ready, 1)

            extras = dve.value_load(tab[0:1, NW:NW + 1], min_val=0, max_val=MAXG)
            with dve.If(extras < 1):
                windows(False)
            with dve.Else():
                windows(True)
            end_phase(dve, 1)

            flat = [counts[:, x, :, :].rearrange("p k n -> p (k n)") for x in range(4)]
            def copy_v_rows(i):
                n2 = 2 * WT_HALVES[i][0].heads
                dve.wait_ge(v_done, 1 + i + 1)
                v.tensor_copy(v_rows[i % 2][0:n2, :], ps[0:n2, 6 * 512:6 * 512 + D // 2]).then_inc(v_copied, 1)

            def total_counts():
                link(v.tensor_tensor(flat[TOTAL], flat[0], flat[1], ALU.add))
                link(v.tensor_tensor(flat[TOTAL], flat[TOTAL], flat[2], ALU.add))
                for k in range(T):
                    o = counts[:, TOTAL, k, k * P:(k + 1) * P]
                    last = v.tensor_tensor(o, o, identb[:, :], ALU.add)
                link(last)

            for i in range(3):
                copy_v_rows(i)
            for q in range(8):
                if q >= 2:
                    copy_v_rows(3 + q - 2)
                    dve.wait_ge(nm_turned, (q - 1) * (T // 2))
                v.tensor_scalar(nomask_h[q % 2], counts[:, q // 2, :, q % 2 * MH:(q % 2 + 1) * MH], 0.0, BIG,
                                ALU.is_equal, ALU.mult).then_inc(nm_ready, 1)
                if q == 2:
                    total_counts()
            for i in range(9, 12):
                copy_v_rows(i)
            dve.wait_ge(v_turned, 12)
            for i, (c, r, h) in enumerate(WT_HALVES):
                for q in range(2):
                    at = c.v_at + q * c.RH + r * c.heads
                    v.tensor_copy(vtab[:, h * (DT // 2):(h + 1) * (DT // 2), at:at + c.heads],
                                  bank(7, 3 * 2 * c.heads, V_COLS_AT + i * 24).rearrange("p (j q h) -> p j q h", j=DT // 2, q=2)[:, :, q, :])
            end_phase(dve, 2)

            def elu():
                def low(t):
                    if t >= 8:
                        dve.wait_ge(elu_done, t - 7)
                    v.tensor_scalar(spare[t % 8], featv[:, t, :], 0.0, None, ALU.min).then_inc(elu_min, 1)
                low(0)
                low(1)
                for t in range(T):
                    dve.wait_ge(elu_e, t + 1)
                    v.scalar_tensor_tensor(featv[:, t, :], featv[:, t, :], 0.0, spare[t % 8], ALU.max,
                                           ALU.add).then_inc(elu_done, 1)
                    if t + 2 < T:
                        low(t + 2)

            def layer(ci, c, ph):
                s = sems[c]
                H, R, RH = c.heads, c.R, c.RH
                if c is not A:
                    v.tensor_copy(wring[0][:, 0:DT * c.columns(0)].rearrange("p (j c) -> p j c", j=DT)[:, :, c.piece:],
                                  vtab[:, :, c.v_at:c.v_at + 2 * RH]).then_inc(v_in, 1)
                if c is DD:
                    elu()
                n = 0
                for r in range(R):
                    dve.wait_ge(*s.s_in[r % 2].at(16 * (r // 2 + 1)))
                    for t in range(T):
                        dve.wait_ge(*s.nm_in[n % 3].at(16 * (n // 3 + 1)))
                        for h in range(H):
                            if n * H + h >= 2:
                                dve.wait_ge(*s.max_done.at(n * H + h - 1))
                            v.tensor_tensor_reduce(junk[(n * H + h) % 2], sbc[r % 2][:, h, :], nm_in[n % 3], 1.0, -3.0e38,
                                                          ALU.subtract, ALU.max, mx[:, t, r * H + h:r * H + h + 1]) \
                                .then_inc(s.max_done.sem, 1)
                        n += 1
                dve.wait_ge(*s.max_done.at(R * T * H))
                d_ = sd[:, :, RH:2 * RH]
                lv = lk[:, :, 0:RH]
                link(v.tensor_tensor(lv, mx[:, :, 0:RH], d_, ALU.add))
                link(v.scalar_tensor_tensor(lv, lv, 0.2, lv, ALU.mult, ALU.max))
                m = lk[:, :, 0:H]
                for r in range(1, R):
                    link(v.tensor_tensor(mm_[:, :, 0:H], m, lk[:, :, r * H:(r + 1) * H], ALU.max))
                    m = mm_[:, :, 0:H]
                link(v.scalar_tensor_tensor(mx[:, :, 0:H], m, -0.1 * BIG, m, ALU.is_gt, ALU.mult))
                link(v.tensor_scalar(mx[:, :, 0:H], mx[:, :, 0:H], -1.25, None, ALU.mult))
                pqv = pq[:, :, 0:2 * RH].rearrange("p t (c k) -> p t c k", k=2)
                for r in range(R):
                    last = v.scalar_tensor_tensor(pqv[:, :, r * H:(r + 1) * H, 1], sd[:, :, RH + r * H:RH + (r + 1) * H],
                                                  0.25, mx[:, :, 0:H], ALU.mult, ALU.add)
                link(last)
                v.tensor_tensor(pqv[:, :, :, 0], pqv[:, :, :, 1], d_, ALU.add).then_inc(pq_ready, 1)
                end_phase(dve, ph)

                if c is A:
                    dve.sem_inc(s.x_ready.sem, STEP_CREDIT)
                    dve.sem_inc(s.saved.sem, 2 * T)
                v.memset(hx_all[:, :, 0:1], 1.0).then_inc(ones, 1)
                dve.wait_ge(bias_in, 16 * (ci + 1))

                def exponents(n, i, k, rh, slot, uses, lo, n_):
                    dve.wait_ge(*s.p_used.at(n + 1))
                    if k == 0:
                        dve.wait_ge(*s.pq_in[slot].at(uses))
                    v.scalar_tensor_tensor(xe[i % RING][:, 0:n_], pqb[slot][:, 0, lo:lo + n_], sd[:, k, bass.ds(rh, 1)],
                                           pqb[slot][:, 1, lo:lo + n_], ALU.add, ALU.max).then_inc(s.x_ready.sem, 1)

                def weights(n, i, k, rel, lo, n_):
                    dve.wait_ge(*s.exp_done.at(n + 1))
                    v.scalar_tensor_tensor(xe[i % RING][:, 0:n_], xe[i % RING][:, 0:n_], 3.0e38,
                                           counts[:, rel, k, lo:lo + n_], ALU.min, ALU.mult).then_inc(s.p_ready.sem, 1)

                def normalise(z_ap, a, b, two):
                    o = zc[:, a:b].rearrange("p (a b) -> p a b", b=5) if two else zc[:, a:b]
                    if c.eps:
                        return v.tensor_scalar(o, z_ap, EPS_Z, None, ALU.add)
                    return v.tensor_scalar(o, z_ap, 1.0e-30, None, ALU.max)

                return exponents, weights, normalise

            def attention(ci, c, ph):
                s = sems[c]
                H, R = c.heads, c.R
                exponents, weights, normalise = layer(ci, c, ph)
                if c is not DD:
                    body = c.unroll * R
                    S_ = body * T
                    with trips(dve, c) as it:
                        def head_rel(i):
                            m = i // T
                            return m, m // R, m % R

                        def make_x(i):
                            m, u, r = head_rel(i)
                            exponents(it * S_ + i, i, i % T, r * H + it * c.unroll + u, m % 2,
                                      it * (8 * body) + 16 * (m // 2 + 1), 0, NP)

                        def save(u):
                            hi = it * c.unroll + u
                            dve.wait_ge(*s.p_used.at(hi * (R * T) + (RING + R * T)))
                            if c is B:
                                z = ps[:, u % 2 * 1024:u % 2 * 1024 + 1024].rearrange("p (b c) -> p b c", b=2)[:, :, 0:490] \
                                    .rearrange("p b (t c) -> p b t c", c=98)[:, :, :, 0]
                                last = normalise(z, 0, T, True)
                            else:
                                pair = lambda b, n: ps[:, b * 512:(b + n) * 512].rearrange("p (t c) -> p t c", c=256)[:, :, 0]
                                normalise(pair(2 + 3 * (u % 2), 3), 0, T - SHARED, False)
                                last = normalise(pair(0, 2), T - SHARED, T, False)
                            last.then_inc(s.z_done.sem, 1)
                            dve.wait_ge(*s.z_done.at(hi * 2 + 1))
                            v.reciprocal(rz[:, 0:T], zc[:, 0:T]).then_inc(s.z_done.sem, 1)
                            dve.wait_ge(*s.z_done.at(hi * 2 + 2))
                            for t in [*range(T - SHARED, T), *range(T - SHARED)]:
                                a = sums_at(c, t, u)
                                v.scalar_tensor_tensor(featv[:, t, bass.ds(hi * c.width, c.width)],
                                                       a[:, 1:1 + c.width], rz[:, t:t + 1],
                                                       brow[:, bass.ds(hi * c.width, c.width)],
                                                       ALU.mult, ALU.add).then_inc(s.saved.sem, 1)

                        make_x(0)
                        for i in range(S_):
                            if i + 1 < S_:
                                make_x(i + 1)
                            m, u, r = head_rel(i)
                            weights(it * S_ + i, i, i % T, c.rels[r], 0, NP)
                            if i % (R * T) == SAVE_AFTER and i > SAVE_AFTER:
                                save(u - 1)
                        save(c.unroll - 1)
                else:
                    def exps(j):
                        g, r, k = j // (R * T), j // T % R, j % T
                        exponents(j, j, k, r, (g * R + r) % 2, 16 * ((g * R + r) // 2 + 1),
                                  D_GROUPS[g][0] * P, D_GROUPS[g][1] * P)
                    total = len(D_GROUPS) * R * T
                    exps(0)

                    def save(g):
                        t0, nt = D_GROUPS[g]
                        dve.wait_ge(*s.p_used.at(RING + (g + 1) * R * T))
                        for q in range(nt):
                            last = normalise(bank(2 * ((t0 + q) % 4), 1), q, q + 1, False)
                        link(last)
                        link(v.reciprocal(rz[:, 0:nt], zc[:, 0:nt]))
                        for q in range(nt):
                            b = 2 * ((t0 + q) % 4)
                            v.scalar_tensor_tensor(featv[:, t0 + q, 0:384], bank(b, 384, 1), rz[:, q:q + 1],
                                                   brow[:, 0:384], ALU.mult, ALU.add)
                            v.scalar_tensor_tensor(featv[:, t0 + q, 384:768], bank(b + 1, 384), rz[:, q:q + 1],
                                                   brow[:, 384:768], ALU.mult, ALU.add).then_inc(s.saved.sem, 1)

                    def f_stats(t):
                        x = featv[:, t, :]
                        dve.wait_ge(*s.saved.at(2 * T + t + 1))
                        dve.wait_ge(f_x, 16 * (8 if t < 8 else T))
                        link(v.tensor_tensor(x, x, spare[t % 8], ALU.add))
                        norm_stats(x, t, f_std)

                    def f_apply(t):
                        dve.wait_ge(f_sqrt, t + 1)
                        norm_apply(featv[:, t, :], featv[:, t, :], t).then_inc(f_done, 1)

                    for g, (t0, nt) in enumerate(D_GROUPS):
                        for r in range(R):
                            for k in range(T):
                                j = (g * R + r) * T + k
                                if j + 1 < total:
                                    exps(j + 1)
                                weights(j, j, k, c.rels[r], t0 * P, nt * P)
                                if g and r == 0 and k == SAVE_AFTER:
                                    save(g - 1)
                                at = k - SAVE_AFTER - 1
                                if g and r == 0 and 0 < at <= before[1]:
                                    f_apply(before[0] + at - 1)
                                if g and r == 0 and 0 <= at < before[1]:
                                    f_stats(before[0] + at)
                        before = (t0, nt)
                    save(len(D_GROUPS) - 1)
                    for t in range(t0, T):
                        f_stats(t)
                    for t in range(t0, T):
                        f_apply(t)

            attention(0, A, 3)
            end_phase(dve, 4)
            attention(1, B, 5)
            end_phase(dve, 6)

            dve.wait_ge(y_in, 16 * 4)
            for t in range(T):
                rn = P if t < T - 1 else LAST
                x = featv[:, t, :]
                halves = lambda ap: ap.rearrange("p (q c) -> p q c", q=2)
                dve.wait_ge(y_mm, t + 1)
                v.tensor_tensor(halves(x), halves(ps[:, t % 3 * 1024:(t % 3 + 1) * 1024])[:, :, 0:384], halves(brow[:, :]),
                                ALU.add).then_inc(y_mm_used, 1)
                dve.wait_ge(y_mm_used, t + 1)
                dve.wait_ge(y_x, 16 * (8 if t < 8 else T))
                link(v.tensor_tensor(featv[0:rn, t, :], featv[0:rn, t, :], spare[t % 8][0:rn, :], ALU.add))
                norm_stats(x, t, y_std)
                dve.wait_ge(y_sqrt, t + 1)
                norm_apply(x, x, t).then_inc(y_done, 1)
            end_phase(dve, 7)

            attention(2, C, 8)
            end_phase(dve, 9)
            attention(3, DD, 10)


_INPUTS = ["x", "x_t", "src", "dst", "edge_type", "dst_rows", "norm_g", "norm_b", "al1", "al2", "qk1", "qk2",
           "wt_a", "wt_b", "wt_c", "wt_d", "w_a", "w_b", "w_c", "w_d", "Wu", "bias_a", "bias_b", "bias_c",
           "bias_d", "bias_u"]


def kernel(**inputs):
    import concourse.bacc as bacc
    from concourse.bass_utils import run_bass_kernel_spmd

    a = {k: np.asarray(v) for k, v in inputs.items()}
    edges = lambda v: v.reshape(NCH, EC).T
    lay = {
        "x": a["x"], "x_t": a["x"].T,
        "src": edges(a["src"]), "dst": edges(a["dst"]), "edge_type": edges(a["edge_type_3"]),
        "dst_rows": a["dst"].reshape(NCH, EC),
        "norm_g": a["L0_gnn_norm_g"], "norm_b": a["L0_gnn_norm_b"],
        "al1": np.stack([a["L0_gnn_a_src1"], a["L0_gnn_a_dst1"]]).reshape(2, 8, 96).transpose(2, 1, 0),
        "al2": np.stack([a["L0_gnn_a_src2"], a["L0_gnn_a_dst2"]]).reshape(2, 2, 96).transpose(2, 1, 0),
        "qk1": np.concatenate([a["L1_gnn_k1"], a["L1_gnn_q1"]], 1).reshape(DT, P, 8).transpose(1, 0, 2),
        "qk2": np.concatenate([a["L1_gnn_k2"], a["L1_gnn_q2"]], 1).reshape(DT, P, 2).transpose(1, 0, 2),
        "wt_a": a["L0_gnn_W1"].T, "wt_b": a["L0_gnn_W2"].T,
        "wt_c": a["L1_gnn_W1"].transpose(0, 2, 1), "wt_d": a["L1_gnn_W2"].transpose(0, 2, 1),
        "w_a": a["L0_gnn_W1"], "w_b": a["L0_gnn_W2"],
        "w_c": a["L1_gnn_W1"].reshape(RELS * D, D), "w_d": a["L1_gnn_W2"].reshape(RELS * D, D),
        "Wu": a["L0_gnn_Wu"],
        "bias_a": a["L0_gnn_b1"], "bias_b": a["L0_gnn_b2"], "bias_c": a["L1_gnn_b1"], "bias_d": a["L1_gnn_b2"],
        "bias_u": a["L0_gnn_bu"],
    }
    nc = bacc.Bacc("TRN2", target_bir_lowering=False, num_devices=1)
    arrays, t_in = {}, {}
    for name in _INPUTS:
        v = np.ascontiguousarray(lay[name])
        arrays[f"in_{name}"] = v
        t_in[name] = nc.dram_tensor(f"in_{name}", v.shape, mybir.dt.from_np(v.dtype), kind="ExternalInput").ap()
    out = nc.dram_tensor("out", (N, D), F32, kind="ExternalOutput").ap()
    gnn_program(nc, t_in, out)
    r = run_bass_kernel_spmd(nc, [arrays], core_ids=[0])
    return r.results[0]["out"]
```
